# Optimizing a Trainium2 kernel written in Bass

```python
import numpy as np
import jax
import jax.numpy as jnp

def _softmax(x, axis=-1):
    return jax.nn.softmax(x, axis=axis)

def _gelu(x):
    return jax.nn.gelu(x, approximate=True)

def _silu(x):
    return jax.nn.silu(x)

def _sigmoid(x):
    return jax.nn.sigmoid(x)

def _layernorm(x, axis=-1, eps=1e-05):
    m = jnp.mean(x, axis=axis, keepdims=True)
    v = jnp.var(x, axis=axis, keepdims=True)
    return (x - m) / jnp.sqrt(v + eps)

def _scatter_add(tgt, idx, src, axis=0):
    return tgt.at[idx].add(src)

def _segment_sum(src, seg, n):
    return jax.ops.segment_sum(src, seg, n)
kernel_name = 'mk_adaln_d1_jaxref_r8_be7687'

def setup_inputs(seed: int=0):
    np.random.seed(seed)
    _w = jnp.asarray

    def _L0_attn_setup():
        import jax, jax.numpy as jnp
        import numpy as np
        B, T, D = (4, 512, 128)
        HD = 64
        H = D // HD
        C = 64
        key = jax.random.key(seed)
        k1, k2, k3 = jax.random.split(key, 3)
        out = jax.random.normal(k1, (B, T, D), jnp.float32)
        W_write = jax.random.normal(k2, (D, D), jnp.float32) * 0.03
        W_read = jax.random.normal(k3, (D, D), jnp.float32) * 0.03
        decay = jnp.full((H,), 4.6, jnp.float32)
        log_alpha = jnp.log(jnp.full((H,), 0.03, jnp.float32))
        return {'out': out, 'W_write': W_write, 'W_read': W_read, 'decay': decay, 'log_alpha': log_alpha}
    _L0_attn_in = _L0_attn_setup()

    def _L0_ffn_setup():
        import jax, jax.numpy as jnp
        import numpy as np
        S, B, H, F, E, K = (256, 2, 128, 256, 8, 2)

        def _moe_forward(hidden_states, router_w, w1, b1, w2, b2):
            s, b, h = hidden_states.shape
            T = s * b
            x = hidden_states.reshape(T, h)
            logits = jnp.einsum('th,eh->te', x, router_w)
            topk_logits, topk_idx = jax.lax.top_k(logits, K)
            probs = jax.nn.softmax(topk_logits, axis=-1)
            combine = jnp.zeros((T, E), dtype=x.dtype)
            combine = combine.at[jnp.arange(T)[:, None], topk_idx].add(probs.astype(x.dtype))
            hmid = jnp.einsum('th,efh->etf', x, w1) + b1[:, None, :]
            hmid = jax.nn.gelu(hmid, approximate=False)
            y = jnp.einsum('etf,ehf->eth', hmid, w2) + b2[:, None, :]
            out = jnp.einsum('eth,te->th', y, combine)
            return out.reshape(s, b, h)
        key = jax.random.key(seed)
        ks = jax.random.split(key, 6)
        std = 0.02
        return {'hidden_states': jax.random.normal(ks[0], (S, B, H), dtype=jnp.float32), 'router_w': jax.random.normal(ks[1], (E, H), dtype=jnp.float32) * std, 'w1': jax.random.normal(ks[2], (E, F, H), dtype=jnp.float32) * (1.0 / np.sqrt(H)), 'b1': jnp.zeros((E, F), dtype=jnp.float32), 'w2': jax.random.normal(ks[3], (E, H, F), dtype=jnp.float32) * (1.0 / np.sqrt(F)), 'b2': jnp.zeros((E, H), dtype=jnp.float32)}
    _L0_ffn_in = _L0_ffn_setup()
    _L0_c = _w((lambda *s: np.random.randn(*s).astype(np.float32) * 0.05)(16, 128))
    _L0_wmod = _w((lambda *s: np.random.randn(*s).astype(np.float32) * 0.05)(128, 6 * 128) * 128 ** (-0.5))
    _d = {'L0_attn_out': _L0_attn_in['out'], 'L0_attn_W_write': _L0_attn_in['W_write'], 'L0_attn_W_read': _L0_attn_in['W_read'], 'L0_attn_decay': _L0_attn_in['decay'], 'L0_attn_log_alpha': _L0_attn_in['log_alpha'], 'L0_ffn_router_w': _L0_ffn_in['router_w'], 'L0_ffn_w1': _L0_ffn_in['w1'], 'L0_ffn_b1': _L0_ffn_in['b1'], 'L0_ffn_w2': _L0_ffn_in['w2'], 'L0_ffn_b2': _L0_ffn_in['b2'], 'L0_c': _L0_c, 'L0_wmod': _L0_wmod}
    _x0 = _d['L0_attn_out']
    _d['L0_attn_out'] = jax.random.normal(jax.random.fold_in(jax.random.key(seed), 1), (16, 512, 128), dtype=_x0.dtype)
    del _x0
    return _d

def reference(L0_attn_out, L0_attn_W_write, L0_attn_W_read, L0_attn_decay, L0_attn_log_alpha, L0_ffn_router_w, L0_ffn_w1, L0_ffn_b1, L0_ffn_w2, L0_ffn_b2, L0_c, L0_wmod):

    def _L0_attn_ref(out, W_write, W_read, decay, log_alpha):
        import jax, jax.numpy as jnp
        import numpy as np
        B, T, D = (4, 512, 128)
        HD = 64
        H = D // HD
        C = 64
        Bb, Tt, Dd = out.shape
        d, Hh, Cc = (HD, D // HD, C)
        out32 = out.astype(jnp.float32)
        gamma = jax.nn.sigmoid(decay)
        log_gamma = jnp.log(gamma)
        v = (out32 @ W_write.T).reshape(Bb, Tt, Hh, d).transpose(0, 2, 1, 3)
        rk = out32.reshape(Bb, Tt, Hh, d).transpose(0, 2, 1, 3)
        wk = jnp.pad(rk[:, :, :-1], ((0, 0), (0, 0), (1, 0), (0, 0)))
        BH = Bb * Hh
        gamma_bh = jnp.tile(gamma, Bb)
        log_gamma_bh = jnp.tile(log_gamma, Bb)
        nC = Tt // Cc
        v_ch = v.reshape(BH, nC, Cc, d).transpose(1, 0, 2, 3)
        rk_ch = rk.reshape(BH, nC, Cc, d).transpose(1, 0, 2, 3)
        wk_ch = wk.reshape(BH, nC, Cc, d).transpose(1, 0, 2, 3)
        p = jnp.arange(Cc)
        diffs = jnp.clip(p[:, None] - 1 - p[None, :], 0)
        causal = p[:, None] > p[None, :]
        M = jnp.exp(diffs[None].astype(jnp.float32) * log_gamma_bh[:, None, None]) * causal[None]
        g_p = gamma_bh[:, None] ** p[None, :].astype(jnp.float32)
        g_w = gamma_bh[:, None] ** (Cc - 1 - p)[None, :].astype(jnp.float32)
        g_C = gamma_bh ** Cc

        def scan_fn(W, chunk):
            rk_c, wk_c, v_c = chunk
            inter = jnp.einsum('bij,bcj->bci', W, rk_c) * g_p[:, :, None]
            S = jnp.einsum('bcd,bkd->bck', rk_c, wk_c)
            intra = jnp.einsum('bck,bkd->bcd', S * M, v_c)
            W_new = g_C[:, None, None] * W + jnp.einsum('bci,bcj->bij', v_c * g_w[:, :, None], wk_c)
            return (W_new, inter + intra)
        W0 = jnp.zeros((BH, d, d), jnp.float32)
        _, reads = jax.lax.scan(scan_fn, W0, (rk_ch, wk_ch, v_ch))
        reads = reads.transpose(1, 0, 2, 3).reshape(Bb, Hh, Tt, d)
        alpha = jnp.exp(log_alpha)[None, :, None, None]
        reads = (alpha * reads).transpose(0, 2, 1, 3).reshape(Bb, Tt, Dd)
        return out + (reads @ W_read.T).astype(out.dtype)

    def _L0_ffn_ref(hidden_states, router_w, w1, b1, w2, b2):
        import jax, jax.numpy as jnp
        import numpy as np
        S, B, H, F, E, K = (256, 2, 128, 256, 8, 2)

        def _moe_forward(hidden_states, router_w, w1, b1, w2, b2):
            s, b, h = hidden_states.shape
            T = s * b
            x = hidden_states.reshape(T, h)
            logits = jnp.einsum('th,eh->te', x, router_w)
            topk_logits, topk_idx = jax.lax.top_k(logits, K)
            probs = jax.nn.softmax(topk_logits, axis=-1)
            combine = jnp.zeros((T, E), dtype=x.dtype)
            combine = combine.at[jnp.arange(T)[:, None], topk_idx].add(probs.astype(x.dtype))
            hmid = jnp.einsum('th,efh->etf', x, w1) + b1[:, None, :]
            hmid = jax.nn.gelu(hmid, approximate=False)
            y = jnp.einsum('etf,ehf->eth', hmid, w2) + b2[:, None, :]
            out = jnp.einsum('eth,te->th', y, combine)
            return out.reshape(s, b, h)
        return _moe_forward(hidden_states, router_w, w1, b1, w2, b2)
    x = L0_attn_out
    mod = (_silu(L0_c) @ L0_wmod).reshape(L0_c.shape[0], 6, 1, -1)
    sa, ca, ga, sb, cb, gb = (mod[:, 0], mod[:, 1], mod[:, 2], mod[:, 3], mod[:, 4], mod[:, 5])
    ga = (2 * (ga >= 0) - 1) * jnp.maximum(jnp.abs(ga), 0.25)
    gb = (2 * (gb >= 0) - 1) * jnp.maximum(jnp.abs(gb), 0.25)
    h = _layernorm(x, axis=-1) * (1 + ca) + sa
    x = x + ga * _L0_attn_ref(h, L0_attn_W_write, L0_attn_W_read, L0_attn_decay, L0_attn_log_alpha)
    h = _layernorm(x, axis=-1) * (1 + cb) + sb
    x = x + gb * _L0_ffn_ref(h, L0_ffn_router_w, L0_ffn_w1, L0_ffn_b1, L0_ffn_w2, L0_ffn_b2)
    return x

_drawn_inputs = setup_inputs


def setup_inputs(seed=0):
    import zlib

    import numpy as np

    out = dict(_drawn_inputs(seed))
    spreads = {'L0_attn_decay': (4.599999904632568, 0.547),
     'L0_attn_log_alpha': (-3.5065579414367676, 0.6),
     'L0_ffn_b1': (0.0, 0.683),
     'L0_ffn_b2': (0.0, 0.476)}
    factors = {}
    for name, (base, spread) in spreads.items():
        noise = np.random.default_rng([zlib.crc32(name.encode()), seed]).standard_normal(out[name].shape)
        drawn = base * np.exp(spread * noise) if base else spread * noise
        out[name] = jnp.asarray(drawn.astype(out[name].dtype))
    for name, factor in factors.items():
        out[name] = (out[name] * factor).astype(out[name].dtype)
    return out
```

```python
from contextlib import ExitStack

import concourse.bass as bass
from concourse import mybir

F32 = mybir.dt.float32
F32R = mybir.dt.float32r
U32 = mybir.dt.uint32
ALU = mybir.AluOpType
ACT = mybir.ActivationFunctionType

P = 128
EPS = 1e-5
GATE_FLOOR = 0.25
E_CONST = 2.718281828459045
SA, CA, GA, SB, CB, GB = range(6)
HALVES = 2


class Batch:

    def __init__(self, pair, k=0):
        self.n = pair * 2 + k
        self.par = k % 2
        self.half = pair + k // 2

    def next(self):
        later = Batch(0, 0)
        later.n, later.par, later.half = self.n + 1, 1 - self.par, self.half + self.par
        return later


def wait(engine, semaphore, value):
    if isinstance(value, int) and value <= 0:
        return
    engine.wait_ge(semaphore, value)


def stand_alone(engine, passed):
    engine.sem_inc(passed, 1)


def adaln_retention_moe(nc, x, w_write, w_read, decay, log_alpha, router_w, w1, b1, w2, b2, c, wmod, out):
    B, T, D = x.shape
    H = decay.shape[0]
    DH = D // H
    E, F = b1.shape
    NC = T // P
    NM = 6
    EH = E * HALVES
    assert D == P and F == HALVES * P and T == 512 and H == 2 and EH == 16 and B % 2 == 0
    LAST = (B - 4) // 2

    combine_dram = nc.dram_tensor("combine_rows", [2, E, T], F32, kind="Internal").ap()

    with ExitStack() as ctx:
        def sb(name, shape, dt=F32):
            return ctx.enter_context(nc.sbuf_tensor(name, shape, dt))

        def psum(name, shape):
            return ctx.enter_context(nc.psum_tensor(name, shape, F32))

        def sem(name):
            return ctx.enter_context(nc.semaphore(name))

        ident = sb("ident", [P, P])
        ones = sb("ones", [P, P])
        minus_half = sb("minus_half", [P, 4])
        eps_tile = sb("eps_tile", [P, 4])
        e_base = sb("e_base", [P, 4])
        lag = sb("lag", [P, NC * P])
        steps = sb("steps", [P, 3 * P])
        back = sb("back", [P, 3 * DH])
        expert_ids = sb("expert_ids", [P, NC, E])
        same_head = sb("same_head", [P, 3, P])
        mask = sb("mask", [P, H, NC * P])
        wk_decay = sb("wk_decay", [P, 3, P])
        rk_decay = sb("rk_decay", [P, 3 * P])
        decay_all = sb("decay_all", [P, H])
        decay_row = sb("decay_row", [P, 1])
        alpha_row = sb("alpha_row", [P, 1])
        dtmp = sb("dtmp", [P, 4, 3])
        loggam = sb("loggam", [P, 3])
        chunk_decay = sb("chunk_decay", [P, 1])
        c_sb = sb("c_sb", [B, P])
        silu_c = sb("silu_c", [B, P])
        silu_ct = sb("silu_ct", [P, B])
        wmod_sb = sb("wmod_sb", [P, NM * P])
        mods = sb("mods", [P, B, NM])
        gate_tmp = sb("gate_tmp", [P, 3, B])
        ww_sb = sb("ww_sb", [P, P])
        wr_sb = sb("wr_sb", [P, P])
        rw_sb = sb("rw_sb", [E, P])
        b1_sb = sb("b1_sb", [EH, P])
        b2_sb = sb("b2_sb", [E, P])
        wwt = sb("wwt", [P, P])
        wrt = sb("wrt", [P, P])
        rwt = sb("rwt", [P, E])
        b1t = sb("b1t", [P, EH])
        b2t = sb("b2t", [P, E])
        w1_raw = sb("w1_raw", [P, EH, P])
        w2_raw = sb("w2_raw", [P, E, F])
        w1_hi = sb("w1_hi", [P, EH, P], F32R)
        w1_lo = sb("w1_lo", [P, EH, P], F32R)
        w2_hi = sb("w2_hi", [P, EH, P], F32R)
        w2_lo = sb("w2_lo", [P, EH, P], F32R)
        cur = sb("cur", [P, 2, NM])
        x_in = sb("x_in", [P, 2, T])
        stats = sb("stats", [P, 2, NC, 6])
        moments = sb("moments", [P, 2, NC, 2])
        var_eps = sb("var_eps", [P, 2, NC])
        rstd = sb("rstd", [P, 2, NC])
        xhat = sb("xhat", [P, 2, T])
        h_t = sb("h_t", [P, 1 + T])
        ga_h = sb("ga_h", [P, T])
        v_sb = sb("v_sb", [P, T])
        kept = sb("kept", [P, H, T])
        wk_g = sb("wk_g", [P, 3 * P])
        rk_g = sb("rk_g", [P, 3 * P])
        state = sb("state", [P, 3, P])
        r_t = sb("r_t", [P, T])
        z_t = sb("z_t", [P, T])
        x1 = sb("x1", [P, 2, T])
        h2 = sb("h2", [P, T])
        h2_hi = sb("h2_hi", [P, 2, T], F32R)
        h2_lo = sb("h2_lo", [P, 2, T], F32R)
        logits = sb("logits", [P, NC, E])
        top_val = sb("top_val", [P, NC, 8])
        top_idx = sb("top_idx", [P, NC, 8], U32)
        top_f = sb("top_f", [P, NC, 2])
        gap = sb("gap", [P, NC])
        gap_exp = sb("gap_exp", [P, NC])
        gap_sum = sb("gap_sum", [P, NC])
        probs = sb("probs", [P, 2, NC])
        hot = sb("hot", [P, 2, NC, E])
        combine = sb("combine", [P, NC, E])
        combine_t = sb("combine_t", [NC * E, P])
        combine_all = sb("combine_all", [P, 2, E, T])
        g = sb("g", [P, 4, T])
        g_hi = sb("g_hi", [P, 4, T], F32R)
        g_lo = sb("g_lo", [P, 4, T], F32R)
        y_w = sb("y_w", [P, 2, T])
        y_sum = sb("y_sum", [P, T])
        f_t = sb("f_t", [P, T])
        out_sb = sb("out_sb", [P, 2, T])

        ps_mid = [psum(f"ps_mid{i}", [P, T]) for i in range(2)]
        ps_y = [psum(f"ps_y{i}", [P, T]) for i in range(2)]
        bank0 = psum("bank0", [P, T])
        bank1 = psum("bank1", [P, T])
        bank2 = psum("bank2", [P, T])
        bank3 = psum("bank3", [P, T])

        N_SMALL = 12
        s_small = sem("small_loaded")
        s_w1_in = sem("w1_loaded")
        s_w2_in = sem("w2_loaded")
        s_pool = sem("pool_const")
        s_act = sem("act_const")
        s_dve = sem("dve_const")
        s_dve0 = sem("dve_setup_steps")
        s_turn = sem("weights_turned")
        s_hi = sem("weights_hi")
        s_lo = sem("weights_lo")

        with nc.Block() as block:
            @block.sync
            def _(sp):
                sp.dma_start(c_sb[:], c).then_inc(s_small, 16)
                for h in range(H):
                    rows = slice(h * DH, (h + 1) * DH)
                    sp.dma_start(decay_row[rows, :], decay[h:h + 1].partition_broadcast(DH)).then_inc(s_small, 16)
                    sp.dma_start(alpha_row[rows, :], log_alpha[h:h + 1].partition_broadcast(DH)).then_inc(s_small, 16)
                sp.dma_start(decay_all[:], decay.partition_broadcast(P)).then_inc(s_small, 16)
                sp.dma_start(wmod_sb[:], wmod).then_inc(s_small, 16)
                for dst, src in ((ww_sb, w_write), (wr_sb, w_read), (rw_sb, router_w), (b2_sb, b2)):
                    sp.dma_start(dst[:], src).then_inc(s_small, 16)
                sp.dma_start(b1_sb[:], b1.rearrange("e (a f) -> (e a) f", a=HALVES)).then_inc(s_small, 16)
                for q in range(4):
                    es = slice(4 * q, 4 * q + 4)
                    sp.dma_start(w1_raw[:, es, :], w1.rearrange("e (a f) h -> f (e a) h", a=HALVES)[:, es, :]).then_inc(s_w1_in, 16)
                    if q == 3:
                        sp.wait_ge(s_w1_in, 64)
                for q in range(4):
                    es = slice(2 * q, 2 * q + 2)
                    sp.dma_start(w2_raw[:, es, :], w2.rearrange("e h f -> h e f")[:, es, :]).then_inc(s_w2_in, 16)
                sp.wait_ge(s_w2_in, 64)

            @block.gpsimd
            def _(pool):
                nc.gpsimd.memset(ones[:], 1.0).then_inc(s_pool, 1)
                nc.gpsimd.memset(minus_half[:], -0.5)
                nc.gpsimd.memset(eps_tile[:], EPS)
                nc.gpsimd.memset(e_base[:], E_CONST)
                nc.gpsimd.iota(lag[:], pattern=[[0, NC], [1, P]], base=-1, channel_multiplier=-1,
                               allow_small_or_imprecise_dtypes=True).then_inc(s_pool, 1)
                nc.gpsimd.iota(steps[:], pattern=[[0, 3], [1, P]], base=0, channel_multiplier=0,
                               allow_small_or_imprecise_dtypes=True)
                nc.gpsimd.iota(back[:], pattern=[[0, 3 * DH]], base=P - 1, channel_multiplier=-1,
                               allow_small_or_imprecise_dtypes=True)
                nc.gpsimd.iota(expert_ids[:], pattern=[[0, NC], [1, E]], base=0, channel_multiplier=0,
                               allow_small_or_imprecise_dtypes=True)
                pool.wait_ge(s_pool, 1)
                nc.gpsimd.affine_select(out=ident[:], in_=ones[:], compare_op=ALU.is_equal, fill=0.0, base=0,
                                        pattern=[[-1, P]], channel_multiplier=1).then_inc(s_pool, 1)
                for h in range(H):
                    pool.wait_ge(s_act, 3 + h)
                    nc.gpsimd.affine_select(out=mask[:, h, :], in_=mask[:, h, :], compare_op=ALU.is_gt, fill=0.0,
                                            base=0, pattern=[[0, NC], [1, P]], channel_multiplier=-1)

            @block.scalar
            def _(act):
                act.wait_ge(s_small, 16 * N_SMALL)
                nc.scalar.activation(dtmp[:, 0, 0:H], decay_all[:], ACT.Exp, scale=-1.0)
                nc.scalar.activation(dtmp[:, 0, H:H + 1], decay_row[:], ACT.Exp, scale=-1.0)
                nc.scalar.activation(alpha_row[:], alpha_row[:], ACT.Exp).then_inc(s_act, 1)
                act.wait_ge(s_dve, 1)
                nc.scalar.activation(loggam[:], dtmp[:, 2, :], ACT.Ln).then_inc(s_act, 1)
                act.wait_ge(s_act, 2)
                act.wait_ge(s_dve, 2)
                for h in range(H):
                    nc.scalar.activation(mask[:, h, :], lag[:], ACT.Exp, scale=loggam[:, h:h + 1]).then_inc(s_act, 1)
                act.wait_ge(s_pool, 3)
                for h in range(H):
                    nc.scalar.activation(wk_decay[:, :, h * DH:(h + 1) * DH],
                                         back[:].rearrange("p (a b) -> p a b", a=3), ACT.Exp,
                                         scale=loggam[:, h:h + 1])
                nc.scalar.activation(rk_decay[:], steps[:], ACT.Exp, scale=loggam[:, H:H + 1])
                nc.scalar.activation(chunk_decay[:], loggam[:, H:H + 1], ACT.Exp, scale=float(P))
                nc.scalar.activation(silu_c[:], c_sb[:], ACT.Silu).then_inc(s_act, 1)
                for q in range(8):
                    act.wait_ge(s_turn, q + 1)
                    dst = (w1_hi if q < 4 else w2_hi)[:, 4 * (q % 4):4 * (q % 4) + 4, :]
                    nc.scalar.activation(dst, [bank0, bank1][q % 2][:].rearrange("p (a b) -> p a b", a=4),
                                         ACT.Copy).then_inc(s_hi, 1)

            @block.tensor
            def _(pe):
                pe.wait_ge(s_pool, 3)
                for q in range(8):
                    if q < 4:
                        pe.wait_ge(s_w1_in, 64)
                    else:
                        pe.wait_ge(s_w2_in, 64)
                    if q >= 2:
                        pe.wait_ge(s_lo, q - 1)
                    for j in range(4):
                        eh = 4 * (q % 4) + j
                        src = w1_raw[:, eh, :] if q < 4 else w2_raw[:, eh // 2, (eh % 2) * P:(eh % 2 + 1) * P]
                        last = nc.tensor.transpose([bank0, bank1][q % 2][:, j * P:(j + 1) * P], src, ident[:])
                    last.then_inc(s_turn, 1)
                pe.wait_ge(s_small, 16 * N_SMALL)
                pe.wait_ge(s_act, 5)
                nc.tensor.transpose(bank2[:, 0:P], ww_sb[:], ident[:])
                nc.tensor.transpose(bank2[:, P:2 * P], wr_sb[:], ident[:])
                nc.tensor.transpose(bank2[:, 256:256 + E], rw_sb[:], ident[0:E, 0:E])
                nc.tensor.transpose(bank2[:, 272:272 + EH], b1_sb[:], ident[0:EH, 0:EH])
                nc.tensor.transpose(bank2[:, 288:288 + E], b2_sb[:], ident[0:E, 0:E])
                nc.tensor.transpose(bank2[:, 304:304 + B], silu_c[:], ident[0:B, 0:B]).then_inc(s_turn, 1)
                pe.wait_ge(s_dve, 3)
                for j in range(NM):
                    last = nc.tensor.matmul(bank3[:, j * B:(j + 1) * B], wmod_sb[:, j * P:(j + 1) * P], silu_ct[:],
                                            start=True, stop=True)
                last.then_inc(s_turn, 1)

            @block.vector
            def _(dve):
                nc.vector.memset(h_t[:, 0:1], 0.0)
                nc.vector.memset(same_head[:], 0.0).then_inc(s_dve0, 1)
                dve.wait_ge(s_dve0, 1)
                for h in range(H):
                    nc.vector.memset(same_head[h * DH:(h + 1) * DH, :, h * DH:(h + 1) * DH], 1.0)
                dve.wait_ge(s_act, 1)
                nc.vector.tensor_scalar(dtmp[:, 1, :], dtmp[:, 0, :], 1.0, None, ALU.add).then_inc(s_dve0, 1)
                dve.wait_ge(s_dve0, 2)
                nc.vector.reciprocal(dtmp[:, 2, :], dtmp[:, 1, :]).then_inc(s_dve, 1)
                dve.wait_ge(s_pool, 2)
                nc.vector.tensor_scalar(lag[:], lag[:], 0.0, None, ALU.max).then_inc(s_dve, 1)
                for q in range(8):
                    dve.wait_ge(s_hi, q + 1)
                    hi, lo = (w1_hi, w1_lo) if q < 4 else (w2_hi, w2_lo)
                    es = slice(4 * (q % 4), 4 * (q % 4) + 4)
                    nc.vector.tensor_tensor(lo[:, es, :], [bank0, bank1][q % 2][:].rearrange("p (a b) -> p a b", a=4),
                                            hi[:, es, :].bitcast(F32), ALU.subtract).then_inc(s_lo, 1)
                dve.wait_ge(s_turn, 9)
                nc.vector.tensor_copy(silu_ct[:], bank2[:, 304:304 + B]).then_inc(s_dve, 1)
                nc.vector.tensor_copy(wwt[:], bank2[:, 0:P])
                nc.vector.tensor_scalar(wrt[:], bank2[:, P:2 * P], alpha_row[:], None, ALU.mult)
                nc.vector.tensor_copy(rwt[:], bank2[:, 256:256 + E])
                nc.vector.tensor_copy(b1t[:], bank2[:, 272:272 + EH])
                nc.vector.tensor_copy(b2t[:], bank2[:, 288:288 + E])
                dve.wait_ge(s_turn, 10)
                nc.vector.tensor_copy(mods[:].rearrange("p b j -> p j b"),
                                      bank3[:, 0:NM * B].rearrange("p (j b) -> p j b", j=NM)).then_inc(s_dve0, 1)
                dve.wait_ge(s_dve0, 3)
                n = 3
                for j in (CA, CB):
                    nc.vector.tensor_scalar(mods[:, :, j], mods[:, :, j], 1.0, None, ALU.add)
                for j in (GA, GB):
                    nc.vector.tensor_scalar(gate_tmp[:, 0, :], mods[:, :, j], -1.0, None, ALU.mult)
                    nc.vector.tensor_scalar(gate_tmp[:, 1, :], mods[:, :, j], 0.0, 2.0, ALU.is_ge,
                                            ALU.mult).then_inc(s_dve0, 1)
                    n += 1
                    dve.wait_ge(s_dve0, n)
                    nc.vector.tensor_tensor(gate_tmp[:, 2, :], gate_tmp[:, 0, :], mods[:, :, j],
                                            ALU.max).then_inc(s_dve0, 1)
                    n += 1
                    dve.wait_ge(s_dve0, n)
                    nc.vector.tensor_scalar(gate_tmp[:, 0, :], gate_tmp[:, 2, :], GATE_FLOOR, None,
                                            ALU.max).then_inc(s_dve0, 1)
                    n += 1
                    dve.wait_ge(s_dve0, n)
                    nc.vector.scalar_tensor_tensor(out=mods[:, :, j], in0=gate_tmp[:, 1, :], scalar=-1.0,
                                                   in1=gate_tmp[:, 0, :], op0=ALU.add,
                                                   op1=ALU.mult).then_inc(s_dve0, 1)
                    n += 1
                    dve.wait_ge(s_dve0, n)

        x_loaded = [sem(f"x_loaded{i}") for i in range(2)]
        combine_loaded = [sem(f"combine_loaded{i}") for i in range(2)]
        out_stored = [sem(f"out_stored{i}") for i in range(2)]
        combine_stored = sem("combine_stored")
        xhat_turned = sem("xhat_turned")
        scores_ready = sem("scores_ready")
        wk_turned = sem("wk_turned")
        values_ready = sem("values_ready")
        updates_ready = sem("updates_ready")
        reads_ready = sem("reads_ready")
        mixed_ready = sem("mixed_ready")
        z_turned = sem("z_turned")
        xhat2_turned = sem("xhat2_turned")
        logits_ready = sem("logits_ready")
        combine_turned = sem("combine_turned")
        ffn_turned = sem("ffn_turned")
        mid_ready = sem("mid_ready")
        y_parts = sem("y_parts")
        h_ready = sem("h_ready")
        values_copied = sem("values_copied")
        reads_copied = sem("reads_copied")
        h2_ready = sem("h2_ready")
        h2_hi_ready = sem("h2_hi_ready")
        combine_copied = sem("combine_copied")
        g_ready = sem("g_ready")
        g_hi_ready = sem("g_hi_ready")
        cur_ready = sem("cur_ready")
        ln_stats = sem("ln_stats")
        ln_moments = sem("ln_moments")
        xhat_ready = sem("xhat_ready")
        scores_masked = sem("scores_masked")
        wk_scaled = sem("wk_scaled")
        updates_masked = sem("updates_masked")
        states_ready = sem("states_ready")
        z_ready = sem("z_ready")
        x1_ready = sem("x1_ready")
        xhat2_ready = sem("xhat2_ready")
        h2_lo_ready = sem("h2_lo_ready")
        logits_copied = sem("logits_copied")
        router_step = sem("router_step")
        dve_passed = sem("dve_passed")
        sp_passed = sem("sp_passed")
        gap_ready = sem("gap_ready")
        hot_scaled = sem("hot_scaled")
        combine_ready = sem("combine_ready")
        g_lo_ready = sem("g_lo_ready")
        y_weighted = sem("y_weighted")
        f_scaled = sem("f_scaled")
        out_ready = sem("out_ready")
        eps_added = sem("eps_added")
        rstd_ready = sem("rstd_ready")
        rk_scaled = sem("rk_scaled")
        ga_h_ready = sem("ga_h_ready")
        gap_exp_ready = sem("gap_exp_ready")
        y_added = sem("y_added")
        ROUTER_STEPS = 7

        x_rows = x.rearrange("b (c p) d -> b p c d", p=P)
        out_rows = out.rearrange("b (c p) d -> b p c d", p=P)

        def chunks(ap):
            return ap.rearrange("p (c d) -> p c d", d=P)

        def run_slots(engine, slot):
            slot(None, Batch(0, 0), None)
            slot(Batch(0, 0), Batch(0, 1), None)
            slot(Batch(0, 1), Batch(0, 2), Batch(0, 0))
            slot(Batch(0, 2), Batch(0, 3), Batch(0, 1))
            with engine.Fori(1, LAST, 1) as pair:
                for k in (1, 2):
                    slot(Batch(pair, k), Batch(pair, k + 1), Batch(pair, k - 1))
            for k in (1, 2, 3):
                b = Batch(LAST, k)
                slot(b, b.next() if b.n < B - 1 else None, Batch(LAST, k - 1))
            slot(None, None, Batch(LAST, 3))

        with nc.Block() as block:
            @block.sync
            def _(sp):
                def hold(semaphore, value):
                    wait(sp, semaphore, value)
                    stand_alone(sp, sp_passed)

                def load_x(a):
                    hold(x1_ready, a.n - 1)
                    sp.dma_start(chunks(x_in[:, a.par, :]), x_rows[a.n]).then_inc(x_loaded[a.par], 16)

                def store(f):
                    hold(out_ready, f.n + 1)
                    sp.dma_start(out_rows[f.n], chunks(out_sb[:, f.par, :])).then_inc(out_stored[f.par], 16)

                def spread_combine(a):
                    hold(combine_copied, a.n + 1)
                    hold(combine_loaded[a.par], 16 * a.half)
                    dst = combine_dram[a.par].rearrange("e (c t) -> c e t", c=NC)
                    for ch in range(NC):
                        sp.dma_start(dst[ch], combine_t[ch * E:(ch + 1) * E, :]).then_inc(combine_stored, 16)
                    hold(combine_stored, 16 * NC * (a.n + 1))
                    hold(y_weighted, E * (a.n - 1))
                    sp.dma_start(combine_all[:, a.par, :, :],
                                 combine_dram[a.par].partition_broadcast(P)).then_inc(combine_loaded[a.par], 16)

                def slot(b, a, f, more=True):
                    if f is not None:
                        store(f)
                    if a is not None:
                        if more:
                            load_x(a.next())
                        spread_combine(a)

                load_x(Batch(0, 0))
                slot(None, Batch(0, 0), None)
                slot(Batch(0, 0), Batch(0, 1), None)
                slot(Batch(0, 1), Batch(0, 2), Batch(0, 0))
                slot(Batch(0, 2), Batch(0, 3), Batch(0, 1))
                with sp.Fori(1, LAST, 1) as pair:
                    for k in (1, 2):
                        slot(Batch(pair, k), Batch(pair, k + 1), Batch(pair, k - 1))
                for k in (1, 2, 3):
                    b = Batch(LAST, k)
                    slot(b, b.next() if b.n < B - 1 else None, Batch(LAST, k - 1), more=b.n + 2 < B)
                store(Batch(LAST, 3))
                for i in range(2):
                    sp.wait_ge(out_stored[i], 16 * (B // 2))

            @block.tensor
            def _(pe):
                mm, turn = nc.tensor.matmul, nc.tensor.transpose

                def w1_block(m, k):
                    if k == 0:
                        pe.wait_ge(h2_hi_ready, m.n + 1)
                        pe.wait_ge(h2_lo_ready, m.n + 1)
                    wait(pe, g_hi_ready, EH * m.n + k - 1)
                    dst = ps_mid[k % 2][:]
                    mm(dst, w1_hi[:, k, :], h2_hi[:, m.par, :], start=True, stop=False)
                    mm(dst, w1_hi[:, k, :], h2_lo[:, m.par, :], start=False, stop=False)
                    mm(dst, w1_lo[:, k, :], h2_hi[:, m.par, :], start=False, stop=True).then_inc(mid_ready, 1)

                def w2_block(b, k):
                    e = k // 2
                    if k % 2 == 0:
                        wait(pe, y_weighted, E * b.n + e - 1)
                    pe.wait_ge(g_lo_ready, EH * b.n + k + 1)
                    dst = ps_y[e % 2][:]
                    mm(dst, w2_hi[:, k, :], g_hi[:, k % 4, :], start=(k % 2 == 0), stop=False)
                    mm(dst, w2_hi[:, k, :], g_lo[:, k % 4, :], start=False, stop=False)
                    mm(dst, w2_lo[:, k, :], g_hi[:, k % 4, :], start=False, stop=(k % 2 == 1)).then_inc(y_parts, 1)

                def turn_four(dst, src, done):
                    for i in range(NC):
                        last = turn(dst[:, i * P:(i + 1) * P], src[:, i * P:(i + 1) * P], ident[:])
                    last.then_inc(done, 1)

                def turn_xhat(a):
                    pe.wait_ge(xhat_ready, a.n + 1)
                    wait(pe, z_ready, a.n)
                    turn_four(bank0, xhat[:, 0, :], xhat_turned)

                def turn_ffn(f):
                    pe.wait_ge(f_scaled, f.n + 1)
                    pe.wait_ge(x1_ready, f.n + 1)
                    turn_four(bank1, f_t, ffn_turned)

                def scores(a):
                    pe.wait_ge(h_ready, a.n + 1)
                    wait(pe, h2_hi_ready, a.n)
                    wait(pe, combine_copied, a.n)
                    for i in range(NC):
                        for h in range(H):
                            rows = slice(h * DH, (h + 1) * DH)
                            last = mm([bank2, bank3][h][:, i * P:(i + 1) * P], h_t[rows, i * P:(i + 1) * P],
                                      h_t[rows, i * P + 1:(i + 1) * P + 1], start=True, stop=True)
                    last.then_inc(scores_ready, 1)
                    for i in range(NC - 1):
                        last = turn(bank0[:, i * P:(i + 1) * P], h_t[:, i * P:(i + 1) * P], ident[:])
                    last.then_inc(wk_turned, 1)

                def values(a):
                    wait(pe, out_ready, a.n - 1)
                    for i in range(NC):
                        last = mm(bank1[:, i * P:(i + 1) * P], h_t[:, i * P + 1:(i + 1) * P + 1], wwt[:],
                                  start=True, stop=True)
                    last.then_inc(values_ready, 1)

                def updates(a):
                    pe.wait_ge(wk_scaled, a.n + 1)
                    pe.wait_ge(values_copied, a.n + 1)
                    pe.wait_ge(scores_masked, a.n + 1)
                    for i in range(NC - 1):
                        last = mm(bank2[:, i * P:(i + 1) * P], wk_g[:, i * P:(i + 1) * P], v_sb[:, i * P:(i + 1) * P],
                                  start=True, stop=True)
                    last.then_inc(updates_ready, 1)

                def reads(a):
                    pe.wait_ge(states_ready, 2 * (a.n + 1))
                    pe.wait_ge(rk_scaled, a.n + 1)
                    for i in range(NC):
                        cols = slice(i * P, (i + 1) * P)
                        if i:
                            mm(bank3[:, cols], state[:, i - 1, :], rk_g[:, (i - 1) * P:i * P], start=True, stop=False)
                        for h in range(H):
                            last = mm(bank3[h * DH:(h + 1) * DH, cols], v_sb[:, i * P + h * DH:i * P + (h + 1) * DH],
                                      kept[:, h, cols], start=(i == 0), stop=True)
                    last.then_inc(reads_ready, 1)

                def mix(a):
                    pe.wait_ge(reads_copied, a.n + 1)
                    mm(bank0[:], wrt[:], r_t[:], start=True, stop=True).then_inc(mixed_ready, 1)

                def turn_z(a):
                    pe.wait_ge(z_ready, a.n + 1)
                    turn_four(bank1, z_t, z_turned)

                def turn_xhat2(a):
                    pe.wait_ge(xhat2_ready, a.n + 1)
                    turn_four(bank2, xhat[:, 1, :], xhat2_turned)

                def router(a):
                    pe.wait_ge(h2_ready, a.n + 1)
                    for i in range(NC):
                        last = mm(bank3[:, i * E:(i + 1) * E], h2[:, i * P:(i + 1) * P], rwt[:], start=True, stop=True)
                    last.then_inc(logits_ready, 1)

                def turn_combine(a):
                    pe.wait_ge(combine_ready, a.n + 1)
                    turn(bank3[0:NC * E, P:2 * P], combine[:].rearrange("p c e -> p (c e)"),
                         ident[:]).then_inc(combine_turned, 1)

                parts = {2: turn_xhat, 4: scores, 5: values, 6: updates, 8: reads, 9: mix, 10: turn_z,
                         12: turn_xhat2, 13: router, 15: turn_combine}

                def slot(b, a, f):
                    for k in range(EH):
                        if b is not None:
                            if k + 2 < EH:
                                w1_block(b, k + 2)
                            elif a is not None:
                                w1_block(a, k + 2 - EH)
                        elif a is not None and k >= EH - 2:
                            w1_block(a, k + 2 - EH)
                        if a is not None and k in parts:
                            parts[k](a)
                        if f is not None and k == 3:
                            turn_ffn(f)
                        if b is not None:
                            w2_block(b, k)

                run_slots(pe, slot)

            @block.scalar
            def _(act):
                def hidden(m, k):
                    s = EH * m.n + k
                    act.wait_ge(mid_ready, s + 1)
                    wait(act, g_lo_ready, s - 3)
                    nc.scalar.activation(g[:, k % 4, :], ps_mid[k % 2][:], ACT.Gelu,
                                         bias=b1t[:, k:k + 1]).then_inc(g_ready, 1)
                    wait(act, y_parts, s - 3)
                    nc.scalar.activation(g_hi[:, k % 4, :], ps_mid[k % 2][:], ACT.Gelu,
                                         bias=b1t[:, k:k + 1]).then_inc(g_hi_ready, 1)

                def modulated_h(a):
                    act.wait_ge(xhat_turned, a.n + 1)
                    act.wait_ge(cur_ready, a.n + 1)
                    wait(act, values_ready, a.n)
                    wait(act, rk_scaled, a.n)
                    wait(act, ga_h_ready, a.n)
                    nc.scalar.activation(h_t[:, 1:1 + T], bank0[:], ACT.Identity, bias=cur[:, a.par, SA:SA + 1],
                                         scale=cur[:, a.par, CA:CA + 1]).then_inc(h_ready, 1)

                def copy_values(a):
                    act.wait_ge(values_ready, a.n + 1)
                    wait(act, reads_ready, a.n)
                    nc.scalar.activation(v_sb[:], bank1[:], ACT.Copy).then_inc(values_copied, 1)

                def copy_reads(a):
                    act.wait_ge(reads_ready, a.n + 1)
                    wait(act, mixed_ready, a.n)
                    nc.scalar.activation(r_t[:], bank3[:], ACT.Copy).then_inc(reads_copied, 1)

                def modulated_h2(a):
                    act.wait_ge(xhat2_turned, a.n + 1)
                    wait(act, logits_ready, a.n)
                    wait(act, h2_lo_ready, a.n)
                    bias, scale = cur[:, a.par, SB:SB + 1], cur[:, a.par, CB:CB + 1]
                    nc.scalar.activation(h2[:], bank2[:], ACT.Identity, bias=bias, scale=scale).then_inc(h2_ready, 1)
                    wait(act, mid_ready, EH * (a.n - 1))
                    nc.scalar.activation(h2_hi[:, a.par, :], bank2[:], ACT.Identity, bias=bias,
                                         scale=scale).then_inc(h2_hi_ready, 1)

                def copy_combine(a):
                    act.wait_ge(combine_turned, a.n + 1)
                    wait(act, combine_stored, 16 * NC * a.n)
                    nc.scalar.activation(combine_t[:], bank3[0:NC * E, P:2 * P], ACT.Copy).then_inc(combine_copied, 1)

                parts = {2: modulated_h, 5: copy_values, 8: copy_reads, 12: modulated_h2, 15: copy_combine}

                def slot(b, a, f):
                    for k in range(EH):
                        if b is not None and k + 2 < EH:
                            hidden(b, k + 2)
                        if a is not None and k in parts and k < EH - 1:
                            parts[k](a)
                        if a is not None and k + 2 >= EH:
                            hidden(a, k + 2 - EH)
                        if a is not None and k == EH - 1:
                            parts[k](a)

                run_slots(act, slot)

            @block.vector
            def _(dve):
                tt, ts, stt = nc.vector.tensor_tensor, nc.vector.tensor_scalar, nc.vector.scalar_tensor_tensor

                def split(m, k):
                    s = EH * m.n + k
                    dve.wait_ge(g_hi_ready, s + 1)
                    wait(dve, y_parts, s - 3)
                    tt(g_lo[:, k % 4, :], g[:, k % 4, :], g_hi[:, k % 4, :].bitcast(F32),
                       ALU.subtract).then_inc(g_lo_ready, 1)

                def weigh(b, e):
                    dve.wait_ge(y_parts, EH * b.n + 2 * e + 2)
                    if e == 0:
                        dve.wait_ge(combine_loaded[b.par], 16 * (b.half + 1))
                    wait(dve, y_added, (E - 1) * b.n + {0: -1, 1: 0, 2: 1}.get(e, e - 2))
                    stt(out=y_w[:, e % 2, :], in0=ps_y[e % 2][:], scalar=b2t[:, e:e + 1],
                        in1=combine_all[:, b.par, e, :], op0=ALU.add, op1=ALU.mult).then_inc(y_weighted, 1)

                def normalize(a, which, src, turned, done):
                    n = 2 * a.n + which + 1
                    for i in range(NC):
                        last = nc.vector.bn_stats(stats[:, which, i, :], src[:, i * P:(i + 1) * P])
                    last.then_inc(ln_stats, 1)
                    dve.wait_ge(ln_stats, n)
                    wait(dve, rstd_ready, n - 2)
                    stand_alone(dve, dve_passed)
                    for i in range(NC):
                        last = nc.vector.bn_aggr(moments[:, which, i, :], stats[:, which, i, :])
                    last.then_inc(ln_moments, 1)
                    dve.wait_ge(rstd_ready, n)
                    wait(dve, turned, a.n)
                    for i in range(NC):
                        last = ts(xhat[:, which, i * P:(i + 1) * P], src[:, i * P:(i + 1) * P],
                                  moments[:, which, i, 0:1], rstd[:, which, i:i + 1], ALU.subtract, ALU.mult)
                    last.then_inc(done, 1)

                def start(a):
                    dve.wait_ge(x_loaded[a.par], 16 * (a.half + 1))
                    wait(dve, f_scaled, a.n - 1)
                    nc.vector.tensor_copy(cur[:, a.par, :], mods[:, a.n, :]).then_inc(cur_ready, 1)
                    normalize(a, 0, x_in[:, a.par, :], xhat_turned, xhat_ready)

                def mask_scores(a):
                    dve.wait_ge(scores_ready, a.n + 1)
                    wait(dve, reads_ready, a.n)
                    tt(kept[:, 0, :], bank2[:], mask[:, 0, :], ALU.mult)
                    tt(kept[:, 1, :], bank3[:], mask[:, 1, :], ALU.mult).then_inc(scores_masked, 1)

                def scale_wk(a):
                    dve.wait_ge(wk_turned, a.n + 1)
                    wait(dve, updates_ready, a.n)
                    tt(chunks(wk_g[:]), chunks(bank0[:, 0:3 * P]), wk_decay[:], ALU.mult).then_inc(wk_scaled, 1)

                def states(a):
                    dve.wait_ge(updates_ready, a.n + 1)
                    wait(dve, reads_ready, a.n)
                    tt(state[:], chunks(bank2[:, 0:3 * P]), same_head[:], ALU.mult).then_inc(updates_masked, 1)
                    dve.wait_ge(updates_masked, a.n + 1)
                    for i in (1, 2):
                        stt(out=state[:, i, :], in0=state[:, i - 1, :], scalar=chunk_decay[:], in1=state[:, i, :],
                            op0=ALU.mult, op1=ALU.add).then_inc(states_ready, 1)
                        dve.wait_ge(states_ready, 2 * a.n + i)

                def gate_mixed(a):
                    dve.wait_ge(mixed_ready, a.n + 1)
                    dve.wait_ge(ga_h_ready, a.n + 1)
                    wait(dve, z_turned, a.n)
                    stt(out=z_t[:], in0=bank0[:], scalar=cur[:, a.par, GA:GA + 1], in1=ga_h[:], op0=ALU.mult,
                        op1=ALU.add).then_inc(z_ready, 1)

                def residual(a):
                    dve.wait_ge(z_turned, a.n + 1)
                    tt(x1[:, a.par, :], x_in[:, a.par, :], bank1[:], ALU.add).then_inc(x1_ready, 1)
                    dve.wait_ge(x1_ready, a.n + 1)
                    normalize(a, 1, x1[:, a.par, :], xhat2_turned, xhat2_ready)

                def split_h2(a):
                    dve.wait_ge(h2_hi_ready, a.n + 1)
                    wait(dve, mid_ready, EH * (a.n - 1))
                    tt(h2_lo[:, a.par, :], h2[:], h2_hi[:, a.par, :].bitcast(F32), ALU.subtract).then_inc(h2_lo_ready, 1)

                def route(a):
                    done = ROUTER_STEPS * a.n
                    dve.wait_ge(logits_ready, a.n + 1)
                    nc.vector.tensor_copy(logits[:], bank3[:, 0:NC * E].rearrange("p (c e) -> p c e", e=E)).then_inc(logits_copied, 1)
                    dve.wait_ge(logits_copied, a.n + 1)
                    wait(dve, gap_ready, a.n)
                    stand_alone(dve, dve_passed)
                    for i in range(NC):
                        last = nc.vector.max(top_val[:, i, :], logits[:, i, :])
                    last.then_inc(router_step, 1)
                    dve.wait_ge(router_step, done + 1)
                    wait(dve, gap_exp_ready, a.n)
                    tt(gap[:], top_val[:, :, 1], top_val[:, :, 0], ALU.subtract).then_inc(gap_ready, 1)
                    for i in range(NC):
                        last = nc.vector.max_index(top_idx[:, i, :], top_val[:, i, :], logits[:, i, :])
                    last.then_inc(router_step, 1)
                    dve.wait_ge(router_step, done + 2)
                    nc.vector.tensor_copy(top_f[:], top_idx[:, :, 0:2]).then_inc(router_step, 1)
                    dve.wait_ge(router_step, done + 3)
                    for j in range(2):
                        last = tt(hot[:, j, :, :], expert_ids[:], top_f[:, :, j:j + 1].to_broadcast([P, NC, E]), ALU.is_equal)
                    last.then_inc(router_step, 1)

                def route_end(a):
                    done = ROUTER_STEPS * a.n
                    dve.wait_ge(gap_exp_ready, a.n + 1)
                    ts(gap_sum[:], gap_exp[:], 1.0, None, ALU.add).then_inc(router_step, 1)
                    dve.wait_ge(router_step, done + 5)
                    nc.vector.reciprocal(probs[:, 0, :], gap_sum[:]).then_inc(router_step, 1)
                    dve.wait_ge(router_step, done + 6)
                    tt(probs[:, 1, :], probs[:, 0, :], gap_exp[:], ALU.mult).then_inc(router_step, 1)
                    dve.wait_ge(router_step, done + 7)
                    for j in range(2):
                        last = tt(hot[:, j, :, :], hot[:, j, :, :],
                                  probs[:, j, :].unsqueeze(2).to_broadcast([P, NC, E]), ALU.mult)
                    last.then_inc(hot_scaled, 1)
                    dve.wait_ge(hot_scaled, a.n + 1)
                    wait(dve, combine_turned, a.n)
                    tt(combine[:], hot[:, 0, :, :], hot[:, 1, :, :], ALU.add).then_inc(combine_ready, 1)

                def scale_ffn(f):
                    dve.wait_ge(y_added, (E - 1) * (f.n + 1))
                    ts(f_t[:], y_sum[:], cur[:, f.par, GB:GB + 1], None, ALU.mult).then_inc(f_scaled, 1)

                def finish(f):
                    dve.wait_ge(ffn_turned, f.n + 1)
                    wait(dve, out_stored[f.par], 16 * f.half)
                    tt(out_sb[:, f.par, :], x1[:, f.par, :], bank1[:], ALU.add).then_inc(out_ready, 1)

                parts = {4: mask_scores, 5: scale_wk, 6: states, 9: gate_mixed, 10: residual, 12: split_h2,
                         13: route, 15: route_end}

                def slot(b, a, f):
                    for k in range(EH):
                        if f is not None and k == 0:
                            weigh(f, E - 1)
                        if f is not None and k == 1:
                            scale_ffn(f)
                        if f is not None and k == 3:
                            finish(f)
                        if a is not None and k == 1:
                            start(a)
                        if b is not None and k + 1 < EH:
                            split(b, k + 1)
                        if b is not None and k % 2 == 0 and k:
                            weigh(b, k // 2 - 1)
                        if a is not None and k in parts:
                            parts[k](a)
                        if a is not None and k == EH - 1:
                            split(a, 0)

                run_slots(dve, slot)

            @block.gpsimd
            def _(pool):
                def rstd_of(a, which):
                    n = 2 * a.n + which + 1
                    pool.wait_ge(ln_moments, n)
                    nc.gpsimd.tensor_tensor(var_eps[:, which, :], moments[:, which, :, 1], eps_tile[:],
                                            ALU.add).then_inc(eps_added, 1)
                    pool.wait_ge(eps_added, n)
                    wait(pool, [xhat_ready, xhat2_ready][which], a.n)
                    nc.gpsimd.tensor_tensor(rstd[:, which, :], var_eps[:, which, :], minus_half[:],
                                            ALU.pow).then_inc(rstd_ready, 1)

                def scale_h(a):
                    pool.wait_ge(h_ready, a.n + 1)
                    wait(pool, reads_ready, a.n)
                    wait(pool, z_ready, a.n)
                    nc.gpsimd.tensor_tensor(rk_g[:], h_t[:, 1 + P:1 + T], rk_decay[:], ALU.mult).then_inc(rk_scaled, 1)
                    nc.gpsimd.tensor_scalar(ga_h[:], h_t[:, 1:1 + T], cur[:, a.par, GA:GA + 1], 0.0, ALU.mult,
                                            ALU.add).then_inc(ga_h_ready, 1)

                def exp_gap(a):
                    pool.wait_ge(gap_ready, a.n + 1)
                    wait(pool, combine_ready, a.n)
                    nc.gpsimd.tensor_tensor(gap_exp[:], e_base[:], gap[:], ALU.pow).then_inc(gap_exp_ready, 1)

                def add_y(b, e):
                    n = (E - 1) * b.n + e
                    pool.wait_ge(y_weighted, E * b.n + e + 1)
                    if e == 1:
                        wait(pool, f_scaled, b.n)
                        nc.gpsimd.tensor_tensor(y_sum[:], y_w[:, 0, :], y_w[:, 1, :], ALU.add).then_inc(y_added, 1)
                    else:
                        pool.wait_ge(y_added, n - 1)
                        nc.gpsimd.tensor_tensor(y_sum[:], y_sum[:], y_w[:, e % 2, :], ALU.add).then_inc(y_added, 1)

                def slot(b, a, f):
                    for k in range(EH):
                        if f is not None and k == 0:
                            add_y(f, E - 1)
                        if a is not None and k == 1:
                            rstd_of(a, 0)
                        if a is not None and k == 2:
                            scale_h(a)
                        if b is not None and k % 2 == 0 and k >= 4:
                            add_y(b, k // 2 - 1)
                        if a is not None and k == 10:
                            rstd_of(a, 1)
                        if a is not None and k == 13:
                            exp_gap(a)

                run_slots(pool, slot)


_INS = ["L0_attn_out", "L0_attn_W_write", "L0_attn_W_read", "L0_attn_decay", "L0_attn_log_alpha",
        "L0_ffn_router_w", "L0_ffn_w1", "L0_ffn_b1", "L0_ffn_w2", "L0_ffn_b2", "L0_c", "L0_wmod"]


def kernel(**inputs):
    import numpy as np
    import concourse.bacc as bacc
    from concourse.bass_utils import run_bass_kernel_spmd

    nc = bacc.Bacc("TRN2", target_bir_lowering=False, num_devices=1)
    arrays, args = {}, []
    for name in _INS:
        a = np.ascontiguousarray(inputs[name])
        arrays[f"in_{name}"] = a
        args.append(nc.dram_tensor(f"in_{name}", a.shape, mybir.dt.from_np(a.dtype), kind="ExternalInput").ap())
    shape = inputs["L0_attn_out"].shape
    out = nc.dram_tensor("out_0", shape, F32, kind="ExternalOutput").ap()
    adaln_retention_moe(nc, *args, out)
    r = run_bass_kernel_spmd(nc, [arrays], core_ids=[0])
    return r.results[0]["out_0"]
```

```python
from contextlib import ExitStack

import concourse.bass as bass
from concourse import mybir

F32 = mybir.dt.float32
F32R = mybir.dt.float32r
U32 = mybir.dt.uint32
ALU = mybir.AluOpType
ACT = mybir.ActivationFunctionType

P = 128
EPS = 1e-5
GATE_FLOOR = 0.25
E_CONST = 2.718281828459045
SA, CA, GA, SB, CB, GB = range(6)
HALVES = 2


class Batch:

    def __init__(self, pair, k=0):
        self.n = pair * 2 + k
        self.par = k % 2
        self.half = pair + k // 2

    def next(self):
        later = Batch(0, 0)
        later.n, later.par, later.half = self.n + 1, 1 - self.par, self.half + self.par
        return later


def wait(engine, semaphore, value):
    if isinstance(value, int) and value <= 0:
        return
    engine.wait_ge(semaphore, value)


def stand_alone(engine, passed):
    engine.sem_inc(passed, 1)


def adaln_retention_moe(nc, x, w_write, w_read, decay, log_alpha, router_w, w1, b1, w2, b2, c, wmod, out):
    B, T, D = x.shape
    H = decay.shape[0]
    DH = D // H
    E, F = b1.shape
    NC = T // P
    NM = 6
    EH = E * HALVES
    assert D == P and F == HALVES * P and T == 512 and H == 2 and EH == 16 and B % 2 == 0
    LAST = (B - 4) // 2
    PIECES = 4
    EP = E // PIECES

    combine_dram = nc.dram_tensor("combine_rows", [2, NC, E, P], F32, kind="Internal").ap()

    with ExitStack() as ctx:
        def sb(name, shape, dt=F32):
            return ctx.enter_context(nc.sbuf_tensor(name, shape, dt))

        def psum(name, shape):
            return ctx.enter_context(nc.psum_tensor(name, shape, F32))

        def sem(name):
            return ctx.enter_context(nc.semaphore(name))

        ident = sb("ident", [P, P])
        ones = sb("ones", [P, P])
        minus_half = sb("minus_half", [P, 4])
        eps_tile = sb("eps_tile", [P, 4])
        zeros = sb("zeros", [P, 4])
        e_base = sb("e_base", [P, 4])
        lag = sb("lag", [P, NC * P])
        steps = sb("steps", [P, 3 * P])
        back = sb("back", [P, 3 * DH])
        expert_ids = sb("expert_ids", [P, NC, E])
        same_head = sb("same_head", [P, 3, P])
        mask = sb("mask", [P, H, NC * P])
        wk_decay = sb("wk_decay", [P, 3, P])
        rk_decay = sb("rk_decay", [P, 3 * P])
        decay_all = sb("decay_all", [P, H])
        decay_row = sb("decay_row", [P, 1])
        alpha_row = sb("alpha_row", [P, 1])
        dtmp = sb("dtmp", [P, 4, 3])
        loggam = sb("loggam", [P, 3])
        chunk_decay = sb("chunk_decay", [P, 1])
        c_sb = sb("c_sb", [B, P])
        silu_c = sb("silu_c", [B, 4, P])
        silu_ct = sb("silu_ct", [P, B])
        wmod_sb = sb("wmod_sb", [P, NM * P])
        mods = sb("mods", [P, B, NM])
        gate_tmp = sb("gate_tmp", [P, 2, 4, B])
        ww_sb = sb("ww_sb", [P, P])
        wr_sb = sb("wr_sb", [P, P])
        rw_sb = sb("rw_sb", [E, P])
        b1_sb = sb("b1_sb", [EH, P])
        b2_sb = sb("b2_sb", [E, P])
        wwt = sb("wwt", [P, P])
        wrt = sb("wrt", [P, P])
        rwt = sb("rwt", [P, E])
        b1t = sb("b1t", [P, EH])
        b2t = sb("b2t", [P, E])
        w1_raw = sb("w1_raw", [P, EH, P])
        w2_raw = sb("w2_raw", [P, E, F])
        w1_hi = sb("w1_hi", [P, EH, P], F32R)
        w1_lo = sb("w1_lo", [P, EH, P], F32R)
        w2_hi = sb("w2_hi", [P, EH, P], F32R)
        w2_lo = sb("w2_lo", [P, EH, P], F32R)
        cur = sb("cur", [P, 2, NM])
        x_in = sb("x_in", [P, 2, T])
        stats = sb("stats", [P, 2, NC, 6])
        moments = sb("moments", [P, 2, NC, 2])
        var_eps = sb("var_eps", [P, 2, NC])
        rstd = sb("rstd", [P, 2, NC])
        minus_mean = sb("minus_mean", [P, 2, NC])
        xhat = sb("xhat", [P, 2, T])
        h_t = sb("h_t", [P, 1 + T])
        ga_h = sb("ga_h", [P, T])
        v_sb = sb("v_sb", [P, T])
        kept = sb("kept", [P, H, T])
        wk_g = sb("wk_g", [P, 3 * P])
        rk_g = sb("rk_g", [P, 3 * P])
        state = sb("state", [P, 3, P])
        r_t = sb("r_t", [P, T])
        z_t = sb("z_t", [P, T])
        x1 = sb("x1", [P, 2, T])
        h2 = sb("h2", [P, T])
        h2_hi = sb("h2_hi", [P, 2, T], F32R)
        h2_lo = sb("h2_lo", [P, 2, T], F32R)
        logits = sb("logits", [P, NC, E])
        top_val = sb("top_val", [P, NC, 8])
        top_idx = sb("top_idx", [P, NC, 8], U32)
        top_f = sb("top_f", [P, NC, 2])
        gap = sb("gap", [P, NC])
        gap_exp = sb("gap_exp", [P, NC])
        gap_sum = sb("gap_sum", [P, NC])
        probs = sb("probs", [P, 2, NC])
        hot = sb("hot", [P, 2, NC, E])
        combine = sb("combine", [P, NC, E])
        combine_t = sb("combine_t", [NC * E, P])
        combine_all = sb("combine_all", [P, 2, NC, E, P])
        g = sb("g", [P, 4, T])
        g_hi = sb("g_hi", [P, 4, T], F32R)
        g_lo = sb("g_lo", [P, 4, T], F32R)
        y_w = sb("y_w", [P, 2, T])
        y_sum = sb("y_sum", [P, T])
        f_t = sb("f_t", [P, T])
        out_sb = sb("out_sb", [P, 2, T])

        ps_mid = [psum(f"ps_mid{i}", [P, T]) for i in range(2)]
        ps_y = [psum(f"ps_y{i}", [P, T]) for i in range(2)]
        bank0 = psum("bank0", [P, T])
        bank1 = psum("bank1", [P, T])
        bank2 = psum("bank2", [P, T])
        bank3 = psum("bank3", [P, T])

        N_SMALL = 7
        N_DECAY = 1 + 2 * H
        s_small = sem("small_loaded")
        s_decay = sem("decay_loaded")
        w1_loaded = sem("w1_loaded")
        w2_loaded = sem("w2_loaded")
        x_loaded = [sem(f"x_loaded{i}") for i in range(2)]
        s_pool = sem("pool_const")
        s_act = sem("act_const")
        s_dve = sem("dve_const")
        s_dve0 = sem("dve_setup_steps")
        s_turn = sem("small_weights_turned")
        x_rows = x.rearrange("b (c p) d -> b p c d", p=P)
        out_rows = out.rearrange("b (c p) d -> b p c d", p=P)

        def chunks(ap):
            return ap.rearrange("p (c d) -> p c d", d=P)

        with nc.Block() as block:
            @block.sync
            def _(sp):
                sp.dma_start(c_sb[:], c).then_inc(s_small, 16)
                sp.dma_start(wmod_sb[:], wmod).then_inc(s_small, 16)
                for dst, src in ((ww_sb, w_write), (wr_sb, w_read), (rw_sb, router_w), (b2_sb, b2)):
                    sp.dma_start(dst[:], src).then_inc(s_small, 16)
                sp.dma_start(b1_sb[:], b1.rearrange("e (a f) -> (e a) f", a=HALVES)).then_inc(s_small, 16)
                for a in range(2):
                    sp.dma_start(chunks(x_in[:, a, :]), x_rows[a]).then_inc(x_loaded[a], 16)
                for q in range(4):
                    es = slice(4 * q, 4 * q + 4)
                    sp.dma_start(w1_raw[:, es, :],
                                 w1.rearrange("e (a f) h -> f (e a) h", a=HALVES)[:, es, :]).then_inc(w1_loaded, 16)
                for q in range(4):
                    es = slice(2 * q, 2 * q + 2)
                    sp.dma_start(w2_raw[:, es, :], w2.rearrange("e h f -> h e f")[:, es, :]).then_inc(w2_loaded, 16)

            @block.gpsimd
            def _(pool):
                nc.gpsimd.memset(ones[:], 1.0).then_inc(s_pool, 1)
                nc.gpsimd.memset(minus_half[:], -0.5)
                nc.gpsimd.memset(eps_tile[:], EPS)
                nc.gpsimd.memset(zeros[:], 0.0)
                nc.gpsimd.memset(e_base[:], E_CONST)
                pool.wait_ge(s_pool, 1)
                nc.gpsimd.affine_select(out=ident[:], in_=ones[:], compare_op=ALU.is_equal, fill=0.0, base=0,
                                        pattern=[[-1, P]], channel_multiplier=1).then_inc(s_pool, 1)
                nc.gpsimd.iota(lag[:], pattern=[[0, NC], [1, P]], base=-1, channel_multiplier=-1,
                               allow_small_or_imprecise_dtypes=True).then_inc(s_pool, 1)
                nc.gpsimd.iota(steps[:], pattern=[[0, 3], [1, P]], base=0, channel_multiplier=0,
                               allow_small_or_imprecise_dtypes=True)
                nc.gpsimd.iota(back[:], pattern=[[0, 3 * DH]], base=P - 1, channel_multiplier=-1,
                               allow_small_or_imprecise_dtypes=True)
                nc.gpsimd.iota(expert_ids[:], pattern=[[0, NC], [1, E]], base=0, channel_multiplier=0,
                               allow_small_or_imprecise_dtypes=True).then_inc(s_pool, 1)
                for h in range(H):
                    pool.wait_ge(s_act, 4 + h)
                    nc.gpsimd.affine_select(out=mask[:, h, :], in_=mask[:, h, :], compare_op=ALU.is_gt, fill=0.0,
                                            base=0, pattern=[[0, NC], [1, P]], channel_multiplier=-1)

            @block.scalar
            def _(act):
                act.dma_start(decay_all[:], decay.partition_broadcast(P)).then_inc(s_decay, 16)
                for h in range(H):
                    rows = slice(h * DH, (h + 1) * DH)
                    act.dma_start(decay_row[rows, :], decay[h:h + 1].partition_broadcast(DH)).then_inc(s_decay, 16)
                    act.dma_start(alpha_row[rows, :], log_alpha[h:h + 1].partition_broadcast(DH)).then_inc(s_decay, 16)
                act.wait_ge(s_decay, 16 * N_DECAY)
                nc.scalar.activation(dtmp[:, 0, 0:H], decay_all[:], ACT.Exp, scale=-1.0)
                nc.scalar.activation(dtmp[:, 0, H:H + 1], decay_row[:], ACT.Exp, scale=-1.0)
                nc.scalar.activation(alpha_row[:], alpha_row[:], ACT.Exp).then_inc(s_act, 1)
                act.wait_ge(s_small, 16 * N_SMALL)
                nc.scalar.activation(silu_c[:, 0, :], c_sb[:], ACT.Exp, scale=-1.0).then_inc(s_act, 1)
                act.wait_ge(s_dve, 1)
                nc.scalar.activation(loggam[:], dtmp[:, 2, :], ACT.Ln).then_inc(s_act, 1)
                act.wait_ge(s_act, 3)
                act.wait_ge(s_dve, 2)
                for h in range(H):
                    nc.scalar.activation(mask[:, h, :], lag[:], ACT.Exp, scale=loggam[:, h:h + 1]).then_inc(s_act, 1)
                act.wait_ge(s_pool, 4)
                for h in range(H):
                    nc.scalar.activation(wk_decay[:, :, h * DH:(h + 1) * DH],
                                         back[:].rearrange("p (a b) -> p a b", a=3), ACT.Exp,
                                         scale=loggam[:, h:h + 1])
                nc.scalar.activation(rk_decay[:], steps[:], ACT.Exp, scale=loggam[:, H:H + 1])
                nc.scalar.activation(chunk_decay[:], loggam[:, H:H + 1], ACT.Exp, scale=float(P))

            @block.tensor
            def _(pe):
                pe.wait_ge(s_pool, 2)
                pe.wait_ge(s_small, 16 * N_SMALL)
                nc.tensor.transpose(bank2[:, 0:P], ww_sb[:], ident[:])
                nc.tensor.transpose(bank2[:, P:2 * P], wr_sb[:], ident[:])
                nc.tensor.transpose(bank2[:, 256:256 + E], rw_sb[:], ident[0:E, 0:E])
                nc.tensor.transpose(bank2[:, 272:272 + EH], b1_sb[:], ident[0:EH, 0:EH])
                nc.tensor.transpose(bank2[:, 288:288 + E], b2_sb[:], ident[0:E, 0:E]).then_inc(s_turn, 1)
                pe.wait_ge(s_dve, 3)
                nc.tensor.transpose(bank3[:, NM * B:(NM + 1) * B], silu_c[:, 3, :], ident[0:B, 0:B]).then_inc(s_turn, 1)
                pe.wait_ge(s_dve, 4)
                for j in range(NM):
                    last = nc.tensor.matmul(bank3[:, j * B:(j + 1) * B], wmod_sb[:, j * P:(j + 1) * P], silu_ct[:],
                                            start=True, stop=True)
                last.then_inc(s_turn, 1)

            @block.vector
            def _(dve):
                nc.vector.memset(h_t[:, 0:1], 0.0)
                nc.vector.memset(same_head[:], 0.0).then_inc(s_dve0, 1)
                dve.wait_ge(s_dve0, 1)
                for h in range(H):
                    nc.vector.memset(same_head[h * DH:(h + 1) * DH, :, h * DH:(h + 1) * DH], 1.0)
                dve.wait_ge(s_act, 1)
                nc.vector.tensor_scalar(dtmp[:, 1, :], dtmp[:, 0, :], 1.0, None, ALU.add).then_inc(s_dve0, 1)
                dve.wait_ge(s_dve0, 2)
                nc.vector.reciprocal(dtmp[:, 2, :], dtmp[:, 1, :]).then_inc(s_dve, 1)
                dve.wait_ge(s_pool, 3)
                nc.vector.tensor_scalar(lag[:], lag[:], 0.0, None, ALU.max).then_inc(s_dve, 1)
                dve.wait_ge(s_act, 2)
                nc.vector.tensor_scalar(silu_c[:, 1, :], silu_c[:, 0, :], 1.0, None, ALU.add).then_inc(s_dve0, 1)
                dve.wait_ge(s_dve0, 3)
                nc.vector.reciprocal(silu_c[:, 2, :], silu_c[:, 1, :]).then_inc(s_dve0, 1)
                dve.wait_ge(s_dve0, 4)
                nc.vector.tensor_tensor(silu_c[:, 3, :], silu_c[:, 2, :], c_sb[:], ALU.mult).then_inc(s_dve, 1)
                dve.wait_ge(s_turn, 2)
                nc.vector.tensor_copy(silu_ct[:], bank3[:, NM * B:(NM + 1) * B]).then_inc(s_dve, 1)
                nc.vector.tensor_copy(wwt[:], bank2[:, 0:P])
                nc.vector.tensor_scalar(wrt[:], bank2[:, P:2 * P], alpha_row[:], None, ALU.mult)
                nc.vector.tensor_copy(rwt[:], bank2[:, 256:256 + E])
                nc.vector.tensor_copy(b1t[:], bank2[:, 272:272 + EH])
                nc.vector.tensor_copy(b2t[:], bank2[:, 288:288 + E])
                dve.wait_ge(s_turn, 3)
                nc.vector.tensor_copy(mods[:].rearrange("p b j -> p j b"),
                                      bank3[:, 0:NM * B].rearrange("p (j b) -> p j b", j=NM)).then_inc(s_dve0, 1)
                dve.wait_ge(s_dve0, 5)
                for j in (CA, CB):
                    nc.vector.tensor_scalar(mods[:, :, j], mods[:, :, j], 1.0, None, ALU.add)
                gates = ((0, GA), (1, GB))
                for i, j in gates:
                    nc.vector.tensor_scalar(gate_tmp[:, i, 0, :], mods[:, :, j], -1.0, None, ALU.mult)
                    last = nc.vector.tensor_scalar(gate_tmp[:, i, 1, :], mods[:, :, j], 0.0, 2.0, ALU.is_ge, ALU.mult)
                last.then_inc(s_dve0, 1)
                dve.wait_ge(s_dve0, 6)
                for i, j in gates:
                    last = nc.vector.tensor_tensor(gate_tmp[:, i, 2, :], gate_tmp[:, i, 0, :], mods[:, :, j], ALU.max)
                last.then_inc(s_dve0, 1)
                dve.wait_ge(s_dve0, 7)
                for i, j in gates:
                    last = nc.vector.tensor_scalar(gate_tmp[:, i, 3, :], gate_tmp[:, i, 2, :], GATE_FLOOR, None, ALU.max)
                last.then_inc(s_dve0, 1)
                dve.wait_ge(s_dve0, 8)
                for i, j in gates:
                    nc.vector.scalar_tensor_tensor(out=mods[:, :, j], in0=gate_tmp[:, i, 1, :], scalar=-1.0,
                                                   in1=gate_tmp[:, i, 3, :], op0=ALU.add, op1=ALU.mult)

        combine_loaded = [[sem(f"combine_loaded{i}_{j}") for j in range(PIECES)] for i in range(2)]
        out_stored = [sem(f"out_stored{i}") for i in range(2)]
        combine_stored = sem("combine_stored")
        xhat_turned = sem("xhat_turned")
        scores_ready = sem("scores_ready")
        wk_turned = sem("wk_turned")
        values_ready = sem("values_ready")
        updates_ready = sem("updates_ready")
        reads_ready = sem("reads_ready")
        mixed_ready = sem("mixed_ready")
        z_turned = sem("z_turned")
        xhat2_turned = sem("xhat2_turned")
        logits_ready = sem("logits_ready")
        combine_turned = sem("combine_turned")
        ffn_turned = sem("ffn_turned")
        weights_turned = sem("weights_turned")
        weights_hi = sem("weights_hi")
        weights_lo = sem("weights_lo")
        mid_ready = sem("mid_ready")
        y_parts = sem("y_parts")
        h_ready = sem("h_ready")
        values_copied = sem("values_copied")
        reads_copied = sem("reads_copied")
        h2_ready = sem("h2_ready")
        h2_hi_ready = sem("h2_hi_ready")
        combine_copied = sem("combine_copied")
        g_ready = sem("g_ready")
        g_hi_ready = sem("g_hi_ready")
        cur_ready = sem("cur_ready")
        ln_stats = [sem(f"ln_stats{i}") for i in range(2)]
        ln_moments = [sem(f"ln_moments{i}") for i in range(2)]
        scores_masked = sem("scores_masked")
        wk_scaled = sem("wk_scaled")
        updates_masked = sem("updates_masked")
        states_ready = sem("states_ready")
        z_ready = sem("z_ready")
        x1_ready = sem("x1_ready")
        h2_lo_ready = sem("h2_lo_ready")
        logits_copied = sem("logits_copied")
        router_step = sem("router_step")
        dve_passed = sem("dve_passed")
        sp_passed = sem("sp_passed")
        gap_ready = sem("gap_ready")
        hot_scaled = sem("hot_scaled")
        combine_ready = sem("combine_ready")
        g_lo_ready = sem("g_lo_ready")
        y_weighted = sem("y_weighted")
        f_scaled = sem("f_scaled")
        out_ready = sem("out_ready")
        eps_added = [sem(f"eps_added{i}") for i in range(2)]
        rstd_ready = [sem(f"rstd_ready{i}") for i in range(2)]
        normalized = [sem(f"normalized{i}") for i in range(2)]
        pool_passed = sem("pool_passed")
        rk_scaled = sem("rk_scaled")
        ga_h_ready = sem("ga_h_ready")
        gap_exp_ready = sem("gap_exp_ready")
        y_added = sem("y_added")
        ROUTER_STEPS = 7

        PREPARE = ({11: (0, 1), 12: (2, 3), 14: (4, 5)}, {0: (6, 7)})

        def blocks_of(q):
            hi, lo = (w1_hi, w1_lo) if q < 4 else (w2_hi, w2_lo)
            es = slice(4 * (q % 4), 4 * (q % 4) + 4)
            return (ps_mid + ps_y)[q % 4], hi[:, es, :], lo[:, es, :]

        def run_slots(engine, slot):
            slot(None, None, Batch(0, 0), None, PREPARE[0])
            slot(None, Batch(0, 0), Batch(0, 1), None, PREPARE[1])
            slot(Batch(0, 0), Batch(0, 1), Batch(0, 2), None)
            for k in (1, 2):
                slot(Batch(0, k), Batch(0, k + 1), Batch(0, k + 2), Batch(0, k - 1))
            with engine.Fori(1, LAST, 1) as pair:
                for k in (1, 2):
                    slot(Batch(pair, k), Batch(pair, k + 1), Batch(pair, k + 2), Batch(pair, k - 1))
            slot(Batch(LAST, 1), Batch(LAST, 2), Batch(LAST, 3), Batch(LAST, 0))
            slot(Batch(LAST, 2), Batch(LAST, 3), None, Batch(LAST, 1))
            slot(Batch(LAST, 3), None, None, Batch(LAST, 2))
            slot(None, None, None, Batch(LAST, 3))

        with nc.Block() as block:
            @block.sync
            def _(sp):
                def hold(semaphore, value):
                    wait(sp, semaphore, value)
                    stand_alone(sp, sp_passed)

                def load_x(a):
                    hold(x1_ready, a.n - 1)
                    sp.dma_start(chunks(x_in[:, a.par, :]), x_rows[a.n]).then_inc(x_loaded[a.par], 16)

                def store(f):
                    hold(out_ready, f.n + 1)
                    sp.dma_start(out_rows[f.n], chunks(out_sb[:, f.par, :])).then_inc(out_stored[f.par], 16)

                def spread_combine(a):
                    hold(combine_copied, a.n + 1)
                    for j in range(PIECES):
                        hold(combine_loaded[a.par][j], 16 * a.half)
                    sp.dma_start(combine_dram[a.par].rearrange("c e t -> (c e) t"),
                                 combine_t[:]).then_inc(combine_stored, 16)
                    hold(combine_stored, 16 * (a.n + 1))
                    hold(y_weighted, E * (a.n - 1))
                    for j in range(PIECES):
                        es = slice(j * EP, (j + 1) * EP)
                        sp.dma_start(combine_all[:, a.par, :, es, :],
                                     combine_dram[a.par, :, es, :].partition_broadcast(P)).then_inc(
                                         combine_loaded[a.par][j], 16)

                def slot(b, late, early, f, prepare={}):
                    if f is not None:
                        store(f)
                    if isinstance(late, Batch) and early is not None and not (isinstance(early.n, int) and early.n == B - 1):
                        load_x(early.next())
                    if late is not None:
                        spread_combine(late)

                run_slots(sp, slot)
                for i in range(2):
                    sp.wait_ge(out_stored[i], 16 * (B // 2))

            @block.tensor
            def _(pe):
                mm, turn = nc.tensor.matmul, nc.tensor.transpose

                def w1_block(m, k):
                    if k == 0:
                        if isinstance(m.n, int) and m.n == 0:
                            pe.wait_ge(weights_lo, 8)
                        pe.wait_ge(h2_hi_ready, m.n + 1)
                        pe.wait_ge(h2_lo_ready, m.n + 1)
                    wait(pe, g_hi_ready, EH * m.n + k - 1)
                    dst = ps_mid[k % 2][:]
                    mm(dst, w1_hi[:, k, :], h2_hi[:, m.par, :], start=True, stop=False)
                    mm(dst, w1_hi[:, k, :], h2_lo[:, m.par, :], start=False, stop=False)
                    mm(dst, w1_lo[:, k, :], h2_hi[:, m.par, :], start=False, stop=True).then_inc(mid_ready, 1)

                def w2_block(b, k):
                    e = k // 2
                    if k % 2 == 0:
                        wait(pe, y_weighted, E * b.n + e - 1)
                    pe.wait_ge(g_lo_ready, EH * b.n + k + 1)
                    dst = ps_y[e % 2][:]
                    mm(dst, w2_hi[:, k, :], g_hi[:, k % 4, :], start=(k % 2 == 0), stop=False)
                    mm(dst, w2_hi[:, k, :], g_lo[:, k % 4, :], start=False, stop=False)
                    mm(dst, w2_lo[:, k, :], g_hi[:, k % 4, :], start=False, stop=(k % 2 == 1)).then_inc(y_parts, 1)

                def turn_four(dst, src, done):
                    for i in range(NC):
                        last = turn(dst[:, i * P:(i + 1) * P], src[:, i * P:(i + 1) * P], ident[:])
                    last.then_inc(done, 1)

                def turn_xhat(a):
                    pe.wait_ge(normalized[0], a.n + 1)
                    wait(pe, z_ready, a.n)
                    turn_four(bank0, xhat[:, 0, :], xhat_turned)

                def turn_ffn(f, late):
                    pe.wait_ge(f_scaled, f.n + 1)
                    if late is not None:
                        pe.wait_ge(values_copied, late.n + 1)
                    else:
                        pe.wait_ge(logits_copied, B)
                    turn_four(bank1, f_t, ffn_turned)

                def scores(a):
                    pe.wait_ge(h_ready, a.n + 1)
                    wait(pe, h2_hi_ready, a.n)
                    wait(pe, reads_copied, a.n)
                    for i in range(NC):
                        for h in range(H):
                            rows = slice(h * DH, (h + 1) * DH)
                            last = mm([bank2, bank3][h][:, i * P:(i + 1) * P], h_t[rows, i * P:(i + 1) * P],
                                      h_t[rows, i * P + 1:(i + 1) * P + 1], start=True, stop=True)
                    last.then_inc(scores_ready, 1)
                    for i in range(NC - 1):
                        last = turn(bank0[:, i * P:(i + 1) * P], h_t[:, i * P:(i + 1) * P], ident[:])
                    last.then_inc(wk_turned, 1)

                def values(a):
                    wait(pe, logits_copied, a.n)
                    for i in range(NC):
                        last = mm(bank1[:, i * P:(i + 1) * P], h_t[:, i * P + 1:(i + 1) * P + 1], wwt[:],
                                  start=True, stop=True)
                    last.then_inc(values_ready, 1)

                def updates(a):
                    pe.wait_ge(wk_scaled, a.n + 1)
                    pe.wait_ge(values_copied, a.n + 1)
                    pe.wait_ge(scores_masked, a.n + 1)
                    for i in range(NC - 1):
                        last = mm(bank2[:, i * P:(i + 1) * P], wk_g[:, i * P:(i + 1) * P], v_sb[:, i * P:(i + 1) * P],
                                  start=True, stop=True)
                    last.then_inc(updates_ready, 1)

                def reads(a):
                    pe.wait_ge(states_ready, 2 * (a.n + 1))
                    wait(pe, combine_copied, a.n)
                    pe.wait_ge(rk_scaled, a.n + 1)
                    for i in range(NC):
                        cols = slice(i * P, (i + 1) * P)
                        if i:
                            mm(bank3[:, cols], state[:, i - 1, :], rk_g[:, (i - 1) * P:i * P], start=True, stop=False)
                        for h in range(H):
                            last = mm(bank3[h * DH:(h + 1) * DH, cols], v_sb[:, i * P + h * DH:i * P + (h + 1) * DH],
                                      kept[:, h, cols], start=(i == 0), stop=True)
                    last.then_inc(reads_ready, 1)

                def mix(a):
                    pe.wait_ge(reads_copied, a.n + 1)
                    mm(bank0[:], wrt[:], r_t[:], start=True, stop=True).then_inc(mixed_ready, 1)

                def turn_z(a):
                    pe.wait_ge(z_ready, a.n + 1)
                    wait(pe, out_ready, a.n - 1)
                    turn_four(bank1, z_t, z_turned)

                def turn_xhat2(a):
                    pe.wait_ge(normalized[1], a.n + 1)
                    turn_four(bank2, xhat[:, 1, :], xhat2_turned)

                def router(a):
                    pe.wait_ge(h2_ready, a.n + 1)
                    for i in range(NC):
                        last = mm(bank1[:, i * E:(i + 1) * E], h2[:, i * P:(i + 1) * P], rwt[:], start=True, stop=True)
                    last.then_inc(logits_ready, 1)

                def turn_combine(a, early):
                    pe.wait_ge(combine_ready, a.n + 1)
                    if early is not None:
                        pe.wait_ge(scores_masked, early.n + 1)
                    turn(bank3[0:NC * E, 0:P], combine[:].rearrange("p c e -> p (c e)"),
                         ident[:]).then_inc(combine_turned, 1)

                def turn_weights(q):
                    bank, _, _ = blocks_of(q)
                    pe.wait_ge(w1_loaded if q < 4 else w2_loaded, 64)
                    wait(pe, weights_lo, q - 3)
                    for j in range(4):
                        eh = 4 * (q % 4) + j
                        src = w1_raw[:, eh, :] if q < 4 else w2_raw[:, eh // 2, (eh % 2) * P:(eh % 2 + 1) * P]
                        last = turn(bank[:, j * P:(j + 1) * P], src, ident[:])
                    last.then_inc(weights_turned, 1)

                early_parts = {10: turn_xhat, 12: scores, 13: values, 15: updates}
                late_parts = {1: reads, 3: mix, 5: turn_z, 9: turn_xhat2, 11: router}

                def slot(b, late, early, f, prepare={}):
                    for k in range(EH):
                        for q in prepare.get(k, ()):
                            turn_weights(q)
                        if b is not None and k + 2 < EH:
                            w1_block(b, k + 2)
                        elif late is not None and k + 2 >= EH:
                            w1_block(late, k + 2 - EH)
                        if late is not None and k in late_parts:
                            late_parts[k](late)
                        if early is not None and k in early_parts:
                            early_parts[k](early)
                        if late is not None and k == 14:
                            turn_combine(late, early)
                        if f is not None and k == 3:
                            turn_ffn(f, late)
                        if b is not None:
                            w2_block(b, k)

                run_slots(pe, slot)

            @block.scalar
            def _(act):
                def hidden(m, k):
                    s = EH * m.n + k
                    act.wait_ge(mid_ready, s + 1)
                    wait(act, g_lo_ready, s - 3)
                    nc.scalar.activation(g[:, k % 4, :], ps_mid[k % 2][:], ACT.Gelu,
                                         bias=b1t[:, k:k + 1]).then_inc(g_ready, 1)
                    wait(act, y_parts, s - 3)
                    nc.scalar.activation(g_hi[:, k % 4, :], ps_mid[k % 2][:], ACT.Gelu,
                                         bias=b1t[:, k:k + 1]).then_inc(g_hi_ready, 1)

                def modulated_h(a):
                    act.wait_ge(xhat_turned, a.n + 1)
                    act.wait_ge(cur_ready, a.n + 1)
                    wait(act, values_ready, a.n)
                    wait(act, rk_scaled, a.n)
                    wait(act, ga_h_ready, a.n)
                    nc.scalar.activation(h_t[:, 1:1 + T], bank0[:], ACT.Identity, bias=cur[:, a.par, SA:SA + 1],
                                         scale=cur[:, a.par, CA:CA + 1]).then_inc(h_ready, 1)

                def copy_values(a):
                    act.wait_ge(values_ready, a.n + 1)
                    wait(act, reads_ready, a.n)
                    nc.scalar.activation(v_sb[:], bank1[:], ACT.Copy).then_inc(values_copied, 1)

                def copy_reads(a):
                    act.wait_ge(reads_ready, a.n + 1)
                    wait(act, mixed_ready, a.n)
                    nc.scalar.activation(r_t[:], bank3[:], ACT.Copy).then_inc(reads_copied, 1)

                def modulated_h2(a):
                    act.wait_ge(xhat2_turned, a.n + 1)
                    wait(act, logits_ready, a.n)
                    wait(act, h2_lo_ready, a.n)
                    bias, scale = cur[:, a.par, SB:SB + 1], cur[:, a.par, CB:CB + 1]
                    nc.scalar.activation(h2[:], bank2[:], ACT.Identity, bias=bias, scale=scale).then_inc(h2_ready, 1)
                    wait(act, mid_ready, EH * (a.n - 1))
                    nc.scalar.activation(h2_hi[:, a.par, :], bank2[:], ACT.Identity, bias=bias,
                                         scale=scale).then_inc(h2_hi_ready, 1)

                def copy_combine(a):
                    act.wait_ge(combine_turned, a.n + 1)
                    wait(act, combine_stored, 16 * a.n)
                    nc.scalar.activation(combine_t[:], bank3[0:NC * E, 0:P], ACT.Copy).then_inc(combine_copied, 1)

                def weights_high(q):
                    bank, hi, _ = blocks_of(q)
                    act.wait_ge(weights_turned, q + 1)
                    nc.scalar.activation(hi, chunks(bank[:]), ACT.Copy).then_inc(weights_hi, 1)

                early_parts = {10: modulated_h, 13: copy_values}
                late_parts = {1: copy_reads, 9: modulated_h2, 14: copy_combine}

                def slot(b, late, early, f, prepare={}):
                    for k in range(EH):
                        for q in prepare.get(k, ()):
                            weights_high(q)
                        if b is not None and k + 2 < EH:
                            hidden(b, k + 2)
                        elif late is not None and k + 2 >= EH:
                            hidden(late, k + 2 - EH)
                        if late is not None and k in late_parts:
                            late_parts[k](late)
                        if early is not None and k in early_parts:
                            early_parts[k](early)

                run_slots(act, slot)

            @block.vector
            def _(dve):
                tt, ts, stt = nc.vector.tensor_tensor, nc.vector.tensor_scalar, nc.vector.scalar_tensor_tensor

                def split(m, k):
                    s = EH * m.n + k
                    dve.wait_ge(g_hi_ready, s + 1)
                    wait(dve, y_parts, s - 3)
                    tt(g_lo[:, k % 4, :], g[:, k % 4, :], g_hi[:, k % 4, :].bitcast(F32),
                       ALU.subtract).then_inc(g_lo_ready, 1)

                def weigh(b, e):
                    dve.wait_ge(y_parts, EH * b.n + 2 * e + 2)
                    if e % EP == 0:
                        dve.wait_ge(combine_loaded[b.par][e // EP], 16 * (b.half + 1))
                    wait(dve, y_added, (E - 1) * b.n + {0: -1, 1: 0, 2: 1}.get(e, e - 2))
                    stt(out=chunks(y_w[:, e % 2, :]), in0=chunks(ps_y[e % 2][:]), scalar=b2t[:, e:e + 1],
                        in1=combine_all[:, b.par, :, e, :], op0=ALU.add, op1=ALU.mult).then_inc(y_weighted, 1)

                def statistics(a, which, src):
                    for i in range(NC):
                        last = nc.vector.bn_stats(stats[:, which, i, :], src[:, i * P:(i + 1) * P])
                    last.then_inc(ln_stats[which], 1)

                def aggregate(a, which):
                    dve.wait_ge(ln_stats[which], a.n + 1)
                    wait(dve, normalized[which], a.n)
                    stand_alone(dve, dve_passed)
                    for i in range(NC):
                        last = nc.vector.bn_aggr(moments[:, which, i, :], stats[:, which, i, :])
                    last.then_inc(ln_moments[which], 1)

                def start(a):
                    dve.wait_ge(x_loaded[a.par], 16 * (a.half + 1))
                    wait(dve, z_ready, a.n - 1)
                    nc.vector.tensor_copy(cur[:, a.par, :], mods[:, a.n, :]).then_inc(cur_ready, 1)
                    statistics(a, 0, x_in[:, a.par, :])
                    aggregate(a, 0)

                def mask_scores(a):
                    dve.wait_ge(scores_ready, a.n + 1)
                    wait(dve, reads_ready, a.n)
                    tt(kept[:, 0, :], bank2[:], mask[:, 0, :], ALU.mult)
                    tt(kept[:, 1, :], bank3[:], mask[:, 1, :], ALU.mult).then_inc(scores_masked, 1)

                def scale_wk(a):
                    dve.wait_ge(wk_turned, a.n + 1)
                    wait(dve, updates_ready, a.n)
                    tt(chunks(wk_g[:]), chunks(bank0[:, 0:3 * P]), wk_decay[:], ALU.mult).then_inc(wk_scaled, 1)

                def states(a):
                    dve.wait_ge(updates_ready, a.n + 1)
                    wait(dve, reads_ready, a.n)
                    tt(state[:], chunks(bank2[:, 0:3 * P]), same_head[:], ALU.mult).then_inc(updates_masked, 1)
                    dve.wait_ge(updates_masked, a.n + 1)
                    for i in (1, 2):
                        stt(out=state[:, i, :], in0=state[:, i - 1, :], scalar=chunk_decay[:], in1=state[:, i, :],
                            op0=ALU.mult, op1=ALU.add).then_inc(states_ready, 1)
                        dve.wait_ge(states_ready, 2 * a.n + i)

                def gate_mixed(a):
                    dve.wait_ge(mixed_ready, a.n + 1)
                    dve.wait_ge(ga_h_ready, a.n + 1)
                    wait(dve, z_turned, a.n)
                    stt(out=z_t[:], in0=bank0[:], scalar=cur[:, a.par, GA:GA + 1], in1=ga_h[:], op0=ALU.mult,
                        op1=ALU.add).then_inc(z_ready, 1)

                def residual(a):
                    dve.wait_ge(z_turned, a.n + 1)
                    tt(x1[:, a.par, :], x_in[:, a.par, :], bank1[:], ALU.add).then_inc(x1_ready, 1)
                    dve.wait_ge(x1_ready, a.n + 1)
                    statistics(a, 1, x1[:, a.par, :])
                    aggregate(a, 1)

                def route(a):
                    done = ROUTER_STEPS * a.n
                    dve.wait_ge(logits_ready, a.n + 1)
                    nc.vector.tensor_copy(logits[:], bank1[:, 0:NC * E].rearrange("p (c e) -> p c e", e=E)).then_inc(logits_copied, 1)
                    dve.wait_ge(logits_copied, a.n + 1)
                    wait(dve, gap_ready, a.n)
                    stand_alone(dve, dve_passed)
                    for i in range(NC):
                        last = nc.vector.max(top_val[:, i, :], logits[:, i, :])
                    last.then_inc(router_step, 1)
                    dve.wait_ge(router_step, done + 1)
                    wait(dve, gap_exp_ready, a.n)
                    tt(gap[:], top_val[:, :, 1], top_val[:, :, 0], ALU.subtract).then_inc(gap_ready, 1)

                def route_indices(a):
                    done = ROUTER_STEPS * a.n
                    for i in range(NC):
                        last = nc.vector.max_index(top_idx[:, i, :], top_val[:, i, :], logits[:, i, :])
                    last.then_inc(router_step, 1)
                    dve.wait_ge(router_step, done + 2)
                    nc.vector.tensor_copy(top_f[:], top_idx[:, :, 0:2]).then_inc(router_step, 1)
                    dve.wait_ge(router_step, done + 3)
                    for j in range(2):
                        last = tt(hot[:, j, :, :], expert_ids[:], top_f[:, :, j:j + 1].to_broadcast([P, NC, E]), ALU.is_equal)
                    last.then_inc(router_step, 1)

                def route_end(a):
                    done = ROUTER_STEPS * a.n
                    dve.wait_ge(gap_exp_ready, a.n + 1)
                    ts(gap_sum[:], gap_exp[:], 1.0, None, ALU.add).then_inc(router_step, 1)
                    dve.wait_ge(router_step, done + 5)
                    nc.vector.reciprocal(probs[:, 0, :], gap_sum[:]).then_inc(router_step, 1)
                    dve.wait_ge(router_step, done + 6)
                    tt(probs[:, 1, :], probs[:, 0, :], gap_exp[:], ALU.mult).then_inc(router_step, 1)
                    dve.wait_ge(router_step, done + 7)
                    for j in range(2):
                        last = tt(hot[:, j, :, :], hot[:, j, :, :],
                                  probs[:, j, :].unsqueeze(2).to_broadcast([P, NC, E]), ALU.mult)
                    last.then_inc(hot_scaled, 1)
                    dve.wait_ge(hot_scaled, a.n + 1)
                    wait(dve, combine_turned, a.n)
                    tt(combine[:], hot[:, 0, :, :], hot[:, 1, :, :], ALU.add).then_inc(combine_ready, 1)

                def scale_ffn(f):
                    dve.wait_ge(y_added, (E - 1) * (f.n + 1))
                    ts(f_t[:], y_sum[:], mods[:, f.n, GB:GB + 1], None, ALU.mult).then_inc(f_scaled, 1)

                def finish(f):
                    dve.wait_ge(ffn_turned, f.n + 1)
                    wait(dve, out_stored[f.par], 16 * f.half)
                    tt(out_sb[:, f.par, :], x1[:, f.par, :], bank1[:], ALU.add).then_inc(out_ready, 1)

                def weights_low(q):
                    bank, hi, lo = blocks_of(q)
                    dve.wait_ge(weights_hi, q + 1)
                    tt(lo, chunks(bank[:]), hi.bitcast(F32), ALU.subtract).then_inc(weights_lo, 1)

                early_parts = {1: start, 13: mask_scores, 14: scale_wk, 15: states}
                late_parts = {3: gate_mixed, 5: residual, 11: route, 12: route_indices, 13: route_end}

                def slot(b, late, early, f, prepare={}):
                    for k in range(EH):
                        for q in prepare.get(k, ()):
                            weights_low(q)
                        if b is not None and k + 1 < EH:
                            split(b, k + 1)
                        elif late is not None and k + 1 == EH:
                            split(late, 0)
                        if f is not None and k == 0:
                            weigh(f, E - 1)
                        if b is not None and k % 2 == 0 and k:
                            weigh(b, k // 2 - 1)
                        if f is not None and k == 2:
                            scale_ffn(f)
                        if late is not None and k in late_parts:
                            late_parts[k](late)
                        if early is not None and k in early_parts:
                            early_parts[k](early)
                        if f is not None and k == 3:
                            finish(f)

                run_slots(dve, slot)

            @block.gpsimd
            def _(pool):
                def normalize(a, which, src, turned):
                    pool.wait_ge(ln_moments[which], a.n + 1)
                    nc.gpsimd.tensor_tensor(var_eps[:, which, :], moments[:, which, :, 1], eps_tile[:],
                                            ALU.add).then_inc(eps_added[which], 1)
                    pool.wait_ge(eps_added[which], a.n + 1)
                    nc.gpsimd.tensor_tensor(rstd[:, which, :], var_eps[:, which, :], minus_half[:], ALU.pow)
                    wait(pool, turned, a.n)
                    nc.gpsimd.tensor_tensor(minus_mean[:, which, :], zeros[:], moments[:, which, :, 0],
                                            ALU.subtract).then_inc(rstd_ready[which], 1)
                    pool.wait_ge(rstd_ready[which], a.n + 1)
                    stand_alone(pool, pool_passed)
                    for i in range(NC):
                        last = nc.gpsimd.tensor_scalar(xhat[:, which, i * P:(i + 1) * P], src[:, i * P:(i + 1) * P],
                                                       minus_mean[:, which, i:i + 1], rstd[:, which, i:i + 1],
                                                       ALU.add, ALU.mult)
                    last.then_inc(normalized[which], 1)

                def split_h2(a):
                    pool.wait_ge(h2_hi_ready, a.n + 1)
                    wait(pool, mid_ready, EH * (a.n - 1))
                    nc.gpsimd.tensor_tensor(h2_lo[:, a.par, :], h2[:], h2_hi[:, a.par, :].bitcast(F32),
                                            ALU.subtract).then_inc(h2_lo_ready, 1)

                def scale_h(a):
                    pool.wait_ge(h_ready, a.n + 1)
                    wait(pool, reads_ready, a.n)
                    wait(pool, z_ready, a.n)
                    nc.gpsimd.tensor_tensor(rk_g[:], h_t[:, 1 + P:1 + T], rk_decay[:], ALU.mult).then_inc(rk_scaled, 1)
                    nc.gpsimd.tensor_scalar(ga_h[:], h_t[:, 1:1 + T], cur[:, a.par, GA:GA + 1], 0.0, ALU.mult,
                                            ALU.add).then_inc(ga_h_ready, 1)

                def exp_gap(a):
                    pool.wait_ge(gap_ready, a.n + 1)
                    wait(pool, combine_ready, a.n)
                    nc.gpsimd.tensor_tensor(gap_exp[:], e_base[:], gap[:], ALU.pow).then_inc(gap_exp_ready, 1)

                def add_y(b, e):
                    n = (E - 1) * b.n + e
                    pool.wait_ge(y_weighted, E * b.n + e + 1)
                    if e == 1:
                        wait(pool, f_scaled, b.n)
                        nc.gpsimd.tensor_tensor(y_sum[:], y_w[:, 0, :], y_w[:, 1, :], ALU.add).then_inc(y_added, 1)
                    else:
                        pool.wait_ge(y_added, n - 1)
                        nc.gpsimd.tensor_tensor(y_sum[:], y_sum[:], y_w[:, e % 2, :], ALU.add).then_inc(y_added, 1)

                def slot(b, late, early, f, prepare={}):
                    for k in range(EH):
                        if f is not None and k == 0:
                            add_y(f, E - 1)
                        if b is not None and k % 2 == 0 and k >= 4:
                            add_y(b, k // 2 - 1)
                        if early is not None and k == 1:
                            normalize(early, 0, x_in[:, early.par, :], xhat_turned)
                        if late is not None and k == 5:
                            normalize(late, 1, x1[:, late.par, :], xhat2_turned)
                        if late is not None and k == 9:
                            split_h2(late)
                        if late is not None and k == 11:
                            exp_gap(late)
                        if early is not None and k == 11:
                            scale_h(early)

                run_slots(pool, slot)


_INS = ["L0_attn_out", "L0_attn_W_write", "L0_attn_W_read", "L0_attn_decay", "L0_attn_log_alpha",
        "L0_ffn_router_w", "L0_ffn_w1", "L0_ffn_b1", "L0_ffn_w2", "L0_ffn_b2", "L0_c", "L0_wmod"]


def kernel(**inputs):
    import numpy as np
    import concourse.bacc as bacc
    from concourse.bass_utils import run_bass_kernel_spmd

    nc = bacc.Bacc("TRN2", target_bir_lowering=False, num_devices=1)
    arrays, args = {}, []
    for name in _INS:
        a = np.ascontiguousarray(inputs[name])
        arrays[f"in_{name}"] = a
        args.append(nc.dram_tensor(f"in_{name}", a.shape, mybir.dt.from_np(a.dtype), kind="ExternalInput").ap())
    shape = inputs["L0_attn_out"].shape
    out = nc.dram_tensor("out_0", shape, F32, kind="ExternalOutput").ap()
    adaln_retention_moe(nc, *args, out)
    r = run_bass_kernel_spmd(nc, [arrays], core_ids=[0])
    return r.results[0]["out_0"]
```

```python
from contextlib import ExitStack

import concourse.bass as bass
from concourse import mybir

F32 = mybir.dt.float32
F32R = mybir.dt.float32r
U32 = mybir.dt.uint32
ALU = mybir.AluOpType
ACT = mybir.ActivationFunctionType

P = 128
EPS = 1e-5
GATE_FLOOR = 0.25
E_CONST = 2.718281828459045
SA, CA, GA, SB, CB, GB = range(6)
HALVES = 2


class Batch:

    def __init__(self, pair, k=0):
        self.n = pair * 2 + k
        self.par = k % 2
        self.half = pair + k // 2

    def next(self):
        later = Batch(0, 0)
        later.n, later.par, later.half = self.n + 1, 1 - self.par, self.half + self.par
        return later


def wait(engine, semaphore, value):
    if isinstance(value, int) and value <= 0:
        return
    engine.wait_ge(semaphore, value)


def stand_alone(engine, passed):
    engine.sem_inc(passed, 1)


def adaln_retention_moe(nc, x, w_write, w_read, decay, log_alpha, router_w, w1, b1, w2, b2, c, wmod, out):
    B, T, D = x.shape
    H = decay.shape[0]
    DH = D // H
    E, F = b1.shape
    NC = T // P
    NM = 6
    NG = 3
    EH = E * HALVES
    assert D == P and F == HALVES * P and T == 512 and H == 2 and EH == 16 and B % 2 == 0
    LAST = (B - 4) // 2
    PIECES = 4
    EP = E // PIECES

    gates_dram = nc.dram_tensor("gate_rows_dram", [NG, B, P], F32, kind="Internal").ap()
    combine_dram = nc.dram_tensor("combine_rows", [2, NC, E, P], F32, kind="Internal").ap()

    with ExitStack() as ctx:
        def sb(name, shape, dt=F32):
            return ctx.enter_context(nc.sbuf_tensor(name, shape, dt))

        def psum(name, shape):
            return ctx.enter_context(nc.psum_tensor(name, shape, F32))

        def sem(name):
            return ctx.enter_context(nc.semaphore(name))

        ident = sb("ident", [P, P])
        ones = sb("ones", [P, P])
        minus_half = sb("minus_half", [P, 4])
        eps_tile = sb("eps_tile", [P, 4])
        zeros = sb("zeros", [P, 4])
        e_base = sb("e_base", [P, 4])
        lag = sb("lag", [P, NC * P])
        steps = sb("steps", [P, 3 * P])
        back = sb("back", [P, 3 * DH])
        expert_ids = sb("expert_ids", [P, NC, E])
        same_head = sb("same_head", [P, 3, P])
        mask = sb("mask", [P, H, NC * P])
        wk_decay = sb("wk_decay", [P, 3, P])
        rk_decay = sb("rk_decay", [P, 3 * P])
        decay_all = sb("decay_all", [P, H])
        decay_row = sb("decay_row", [P, 1])
        alpha_row = sb("alpha_row", [P, 1])
        dtmp = sb("dtmp", [P, 4, 3])
        gelu_warm = sb("gelu_warm", [P, 3])
        loggam = sb("loggam", [P, 3])
        chunk_decay = sb("chunk_decay", [P, 1])
        c_sb = sb("c_sb", [B, P])
        silu_c = sb("silu_c", [B, 4, P])
        silu_ct = sb("silu_ct", [P, B])
        wmod_sb = sb("wmod_sb", [P, NM * P])
        mods = sb("mods", [P, B, NM])
        gate_cols = sb("gate_cols", [P, NG, B])
        gate_rows_all = sb("gate_rows_all", [NG * B, P])
        gate_tmp = sb("gate_tmp", [P, 2, 4, B])
        ww_sb = sb("ww_sb", [P, P])
        wr_sb = sb("wr_sb", [P, P])
        rw_sb = sb("rw_sb", [E, P])
        b1_sb = sb("b1_sb", [EH, P])
        b2_sb = sb("b2_sb", [E, P])
        wwt = sb("wwt", [P, P])
        wrt = sb("wrt", [P, P])
        wrt_g = sb("wrt_g", [P, P])
        rwt = sb("rwt", [P, E])
        b1t = sb("b1t", [P, EH])
        b2t = sb("b2t", [P, E])
        w1_raw = sb("w1_raw", [P, EH, P])
        w2_raw = sb("w2_raw", [P, E, F])
        w1_hi = sb("w1_hi", [P, EH, P], F32R)
        w1_lo = sb("w1_lo", [P, EH, P], F32R)
        w2_hi = sb("w2_hi", [P, EH, P], F32R)
        w2_lo = sb("w2_lo", [P, EH, P], F32R)
        cur = sb("cur", [P, 2, NM])
        gate_rows = sb("gate_rows", [P, 2, NG, P])
        x_in = sb("x_in", [P, 2, T])
        stats = sb("stats", [P, 2, NC, 6])
        moments = sb("moments", [P, 2, NC, 2])
        var_eps = sb("var_eps", [P, 2, NC])
        rstd = sb("rstd", [P, 2, NC])
        minus_mean = sb("minus_mean", [P, 2, NC])
        xhat = sb("xhat", [P, 2, T])
        h_t = sb("h_t", [P, T + 1])
        h_tok = sb("h_tok", [P, T])
        x_base = sb("x_base", [P, T])
        v_sb = sb("v_sb", [P, T])
        kept = sb("kept", [P, H, T])
        wk_g = sb("wk_g", [P, 3 * P])
        rk_g = sb("rk_g", [P, 3 * P])
        state = sb("state", [P, 3, P])
        r_t = sb("r_t", [P, T])
        x1 = sb("x1", [P, 2, T])
        h2 = sb("h2", [P, T])
        h2_hi = sb("h2_hi", [P, 2, T], F32R)
        h2_lo = sb("h2_lo", [P, 2, T], F32R)
        logits = sb("logits", [P, NC, E])
        top_val = sb("top_val", [P, NC, 8])
        top_idx = sb("top_idx", [P, NC, 8], U32)
        top_f = sb("top_f", [P, NC, 2])
        gap = sb("gap", [P, NC])
        gap_exp = sb("gap_exp", [P, NC])
        gap_sum = sb("gap_sum", [P, NC])
        probs = sb("probs", [P, 2, NC])
        hot = sb("hot", [P, 2, NC, E])
        combine = sb("combine", [P, NC, E])
        combine_t = sb("combine_t", [NC * E, P])
        combine_all = sb("combine_all", [P, 2, NC, E, P])
        g = sb("g", [P, 4, T])
        g_hi = sb("g_hi", [P, 4, T], F32R)
        g_lo = sb("g_lo", [P, 4, T], F32R)
        y_w = sb("y_w", [P, 2, T])
        y_sum = sb("y_sum", [P, T])
        f_t = sb("f_t", [P, T])
        out_sb = sb("out_sb", [P, 2, T])

        ps_mid = [psum(f"ps_mid{i}", [P, T]) for i in range(2)]
        ps_y = [psum(f"ps_y{i}", [P, T]) for i in range(2)]
        bank0 = psum("bank0", [P, T])
        bank1 = psum("bank1", [P, T])
        bank2 = psum("bank2", [P, T])
        bank3 = psum("bank3", [P, T])

        N_SMALL = 5
        N_DECAY = 1 + 2 * H
        s_small = sem("small_loaded")
        s_c = sem("c_loaded")
        s_wmod = sem("wmod_loaded")
        s_decay = sem("decay_loaded")
        w1_loaded = sem("w1_loaded")
        w2_loaded = sem("w2_loaded")
        x_loaded = [sem(f"x_loaded{i}") for i in range(2)]
        s_pool = sem("pool_const")
        exp_c_ready = sem("exp_c_ready")
        exp_decay_ready = sem("exp_decay_ready")
        log_gamma_ready = sem("log_gamma_ready")
        mask_powers = sem("mask_powers")
        powers_ready = sem("powers_ready")
        silu_ready = sem("silu_ready")
        silu_copied = sem("silu_copied")
        gamma_ready = sem("gamma_ready")
        lag_clipped = sem("lag_clipped")
        small_ready = sem("small_weights_ready")
        s_dve0 = sem("dve_setup_steps")
        s_turn = sem("small_weights_turned")
        s_mask = sem("masks_ready")
        gate_cols_ready = sem("gate_cols_ready")
        gate_rows_turned = sem("gate_rows_turned")
        gate_rows_copied = sem("gate_rows_copied")
        gate_rows_stored = sem("gate_rows_stored")
        rows_loaded = [sem(f"gate_rows_loaded{i}") for i in range(2)]
        x_rows = x.rearrange("b (c p) d -> b p c d", p=P)
        out_rows = out.rearrange("b (c p) d -> b p c d", p=P)

        def chunks(ap):
            return ap.rearrange("p (c d) -> p c d", d=P)

        combine_loaded = [[sem(f"combine_loaded{i}_{j}") for j in range(PIECES)] for i in range(2)]
        out_stored = [sem(f"out_stored{i}") for i in range(2)]
        combine_stored = sem("combine_stored")
        xhat_turned = sem("xhat_turned")
        scores_ready = sem("scores_ready")
        values_ready = sem("values_ready")
        updates_ready = sem("updates_ready")
        reads_ready = sem("reads_ready")
        mixed_ready = sem("mixed_ready")
        xhat2_turned = sem("xhat2_turned")
        logits_ready = sem("logits_ready")
        combine_turned = sem("combine_turned")
        ffn_turned = sem("ffn_turned")
        weights_turned = sem("weights_turned")
        weights_hi = sem("weights_hi")
        weights_lo = sem("weights_lo")
        mid_ready = sem("mid_ready")
        y_parts = sem("y_parts")
        h_ready = sem("h_ready")
        values_copied = sem("values_copied")
        reads_copied = sem("reads_copied")
        h2_ready = sem("h2_ready")
        h2_hi_ready = sem("h2_hi_ready")
        combine_copied = sem("combine_copied")
        g_ready = sem("g_ready")
        g_hi_ready = sem("g_hi_ready")
        cur_ready = sem("cur_ready")
        ln_stats = [sem(f"ln_stats{i}") for i in range(2)]
        ln_moments = [sem(f"ln_moments{i}") for i in range(2)]
        scores_masked = sem("scores_masked")
        wk_scaled = sem("wk_scaled")
        updates_masked = sem("updates_masked")
        states_ready = sem("states_ready")
        x1_ready = sem("x1_ready")
        h2_lo_ready = sem("h2_lo_ready")
        logits_copied = sem("logits_copied")
        router_step = sem("router_step")
        dve_passed = sem("dve_passed")
        sp_passed = sem("sp_passed")
        gap_ready = sem("gap_ready")
        hot_scaled = sem("hot_scaled")
        combine_ready = sem("combine_ready")
        g_lo_ready = sem("g_lo_ready")
        y_weighted = sem("y_weighted")
        f_scaled = sem("f_scaled")
        out_ready = sem("out_ready")
        eps_added = [sem(f"eps_added{i}") for i in range(2)]
        rstd_ready = [sem(f"rstd_ready{i}") for i in range(2)]
        normalized = [sem(f"normalized{i}") for i in range(2)]
        pool_passed = sem("pool_passed")
        rk_scaled = sem("rk_scaled")
        h_tok_step = sem("h_tok_step")
        base_step = sem("base_step")
        wrt_gated = sem("wrt_gated")
        gap_exp_ready = sem("gap_exp_ready")
        y_added = sem("y_added")
        ROUTER_STEPS = 7

        START = 12
        PREPARE = ({}, {0: (0, 1), 1: (2, 3), 6: (4, 5), 7: (6, 7)})
        BUSY_FIRST = 8
        BUSY = ({13: 6, 15: 3}, {0: 3, 1: 3, 2: 5, 8: 13, 9: 5, 11: 4})

        def first(a):
            return isinstance(a.n, int) and a.n == 0

        def blocks_of(q):
            hi, lo = (w1_hi, w1_lo) if q < 4 else (w2_hi, w2_lo)
            es = slice(4 * (q % 4), 4 * (q % 4) + 4)
            return (ps_mid + ps_y)[q % 4], hi[:, es, :], lo[:, es, :]

        def last_one(a):
            return isinstance(a.n, int) and a.n == B - 1

        def last_two(a):
            return isinstance(a.n, int) and a.n >= B - 2

        def do_parts(k, side, *groups):
            for a, table in groups:
                if a is not None:
                    for part in table.get((k, side), ()):
                        part(a)

        def run_slots(engine, slot):
            slot(None, None, Batch(0, 0), None, PREPARE[0], BUSY[0])
            slot(None, Batch(0, 0), Batch(0, 1), None, PREPARE[1], BUSY[1])
            slot(Batch(0, 0), Batch(0, 1), Batch(0, 2), None)
            for k in (1, 2):
                slot(Batch(0, k), Batch(0, k + 1), Batch(0, k + 2), Batch(0, k - 1))
            with engine.Fori(1, LAST, 1) as pair:
                for k in (1, 2):
                    slot(Batch(pair, k), Batch(pair, k + 1), Batch(pair, k + 2), Batch(pair, k - 1))
            slot(Batch(LAST, 1), Batch(LAST, 2), Batch(LAST, 3), Batch(LAST, 0))
            slot(Batch(LAST, 2), Batch(LAST, 3), None, Batch(LAST, 1))
            slot(Batch(LAST, 3), None, None, Batch(LAST, 2))
            slot(None, None, None, Batch(LAST, 3))

        with nc.Block() as block:
            @block.sync
            def _(sp):
                sp.dma_start(c_sb[:], c).then_inc(s_c, 16)
                sp.dma_start(chunks(x_in[:, 0, :]), x_rows[0]).then_inc(x_loaded[0], 16)
                sp.dma_start(wmod_sb[:], wmod).then_inc(s_wmod, 16)
                sp.dma_start(decay_all[:], decay.partition_broadcast(P)).then_inc(s_decay, 16)
                for h in range(H):
                    rows = slice(h * DH, (h + 1) * DH)
                    sp.dma_start(decay_row[rows, :], decay[h:h + 1].partition_broadcast(DH)).then_inc(s_decay, 16)
                    sp.dma_start(alpha_row[rows, :], log_alpha[h:h + 1].partition_broadcast(DH)).then_inc(s_decay, 16)
                for dst, src in ((ww_sb, w_write), (wr_sb, w_read), (rw_sb, router_w), (b2_sb, b2)):
                    sp.dma_start(dst[:], src).then_inc(s_small, 16)
                sp.dma_start(b1_sb[:], b1.rearrange("e (a f) -> (e a) f", a=HALVES)).then_inc(s_small, 16)
                sp.dma_start(chunks(x_in[:, 1, :]), x_rows[1]).then_inc(x_loaded[1], 16)
                for q in range(4):
                    es = slice(4 * q, 4 * q + 4)
                    sp.dma_start(w1_raw[:, es, :],
                                 w1.rearrange("e (a f) h -> f (e a) h", a=HALVES)[:, es, :]).then_inc(w1_loaded, 16)

                def hold(semaphore, value):
                    wait(sp, semaphore, value)
                    stand_alone(sp, sp_passed)

                def load_gate_rows(a):
                    sp.dma_start(gate_rows[:, a.par, :, :],
                                 gates_dram[:, a.n, :].partition_broadcast(P)).then_inc(rows_loaded[a.par], 16)

                def load_x(a):
                    hold(x1_ready, a.n - 1)
                    load_gate_rows(a)
                    sp.dma_start(chunks(x_in[:, a.par, :]), x_rows[a.n]).then_inc(x_loaded[a.par], 16)

                def store(f):
                    hold(out_ready, f.n + 1)
                    sp.dma_start(out_rows[f.n], chunks(out_sb[:, f.par, :])).then_inc(out_stored[f.par], 16)

                def spread_combine(a):
                    hold(combine_copied, a.n + 1)
                    for j in range(PIECES):
                        hold(combine_loaded[a.par][j], 16 * a.half)
                    sp.dma_start(combine_dram[a.par].rearrange("c e t -> (c e) t"),
                                 combine_t[:]).then_inc(combine_stored, 16)
                    hold(combine_stored, 16 * (a.n + 1))
                    hold(y_weighted, E * (a.n - 1))
                    for j in range(PIECES):
                        es = slice(j * EP, (j + 1) * EP)
                        sp.dma_start(combine_all[:, a.par, :, es, :],
                                     combine_dram[a.par, :, es, :].partition_broadcast(P)).then_inc(
                                         combine_loaded[a.par][j], 16)

                def slot(b, late, early, f, prepare={}, busy={}):
                    if f is not None:
                        store(f)
                    if late is not None and early is not None and not last_one(early):
                        load_x(early.next())
                    if late is not None:
                        spread_combine(late)

                hold(gate_rows_copied, 1)
                sp.dma_start(gates_dram.rearrange("j b d -> (j b) d"), gate_rows_all[:]).then_inc(gate_rows_stored, 16)
                hold(gate_rows_stored, 16)
                for k in range(2):
                    load_gate_rows(Batch(0, k))
                for q in range(4):
                    es = slice(2 * q, 2 * q + 2)
                    sp.dma_start(w2_raw[:, es, :], w2.rearrange("e h f -> h e f")[:, es, :]).then_inc(w2_loaded, 16)

                run_slots(sp, slot)
                for i in range(2):
                    sp.wait_ge(out_stored[i], 16 * (B // 2))

            @block.tensor
            def _(pe):
                mm, turn = nc.tensor.matmul, nc.tensor.transpose

                def w1_block(m, k):
                    if k == 0:
                        if first(m):
                            pe.wait_ge(weights_lo, 8)
                        pe.wait_ge(h2_hi_ready, m.n + 1)
                        pe.wait_ge(h2_lo_ready, m.n + 1)
                    wait(pe, g_hi_ready, EH * m.n + k - 1)
                    dst = ps_mid[k % 2][:]
                    mm(dst, w1_hi[:, k, :], h2_hi[:, m.par, :], start=True, stop=False)
                    mm(dst, w1_hi[:, k, :], h2_lo[:, m.par, :], start=False, stop=False)
                    mm(dst, w1_lo[:, k, :], h2_hi[:, m.par, :], start=False, stop=True).then_inc(mid_ready, 1)

                def w2_block(b, k):
                    e = k // 2
                    if k % 2 == 0:
                        wait(pe, y_weighted, E * b.n + e - 1)
                    pe.wait_ge(g_lo_ready, EH * b.n + k + 1)
                    dst = ps_y[e % 2][:]
                    mm(dst, w2_hi[:, k, :], g_hi[:, k % 4, :], start=(k % 2 == 0), stop=False)
                    mm(dst, w2_hi[:, k, :], g_lo[:, k % 4, :], start=False, stop=False)
                    mm(dst, w2_lo[:, k, :], g_hi[:, k % 4, :], start=False, stop=(k % 2 == 1)).then_inc(y_parts, 1)

                def keep_busy(n, bank=ps_y[1]):
                    for _ in range(n):
                        mm(bank[:, 0:P], ident[:], ident[:], start=True, stop=True)

                def turn_four(dst, src, done):
                    for i in range(NC):
                        last = turn(dst[:, i * P:(i + 1) * P], src[:, i * P:(i + 1) * P], ident[:])
                    last.then_inc(done, 1)

                def turn_small_weights():
                    pe.wait_ge(s_small, 16 * N_SMALL)
                    turn(bank2[:, 0:P], ww_sb[:], ident[:])
                    turn(bank2[:, P:2 * P], wr_sb[:], ident[:])
                    turn(bank2[:, 256:256 + E], rw_sb[:], ident[0:E, 0:E])
                    turn(bank2[:, 272:272 + EH], b1_sb[:], ident[0:EH, 0:EH])
                    turn(bank2[:, 288:288 + E], b2_sb[:], ident[0:E, 0:E]).then_inc(s_turn, 1)

                def turn_gates():
                    pe.wait_ge(gate_cols_ready, 1)
                    turn(bank3[0:NG * B, P:2 * P], gate_cols[:].rearrange("p j b -> p (j b)"),
                         ident[:]).then_inc(gate_rows_turned, 1)

                def turn_xhat(a):
                    pe.wait_ge(normalized[0], a.n + 1)
                    wait(pe, x1_ready, a.n)
                    turn_four(bank0, xhat[:, 0, :], xhat_turned)
                    if first(a):
                        turn_small_weights()
                        turn_gates()

                def turn_ffn(f):
                    pe.wait_ge(f_scaled, f.n + 1)
                    if not last_two(f):
                        pe.wait_ge(values_copied, f.n + 3)
                    else:
                        pe.wait_ge(logits_copied, B)
                    turn_four(bank1, f_t, ffn_turned)

                def scores(a):
                    pe.wait_ge(h_ready, a.n + 1)
                    if first(a):
                        pe.wait_ge(gate_rows_copied, 1)
                        pe.wait_ge(small_ready, 1)
                    wait(pe, h2_hi_ready, a.n)
                    wait(pe, reads_copied, a.n)
                    for i in range(NC):
                        for h in range(H):
                            rows = slice(h * DH, (h + 1) * DH)
                            last = mm([bank2, bank3][h][:, i * P:(i + 1) * P], h_t[rows, i * P:(i + 1) * P],
                                      h_t[rows, i * P + 1:(i + 1) * P + 1], start=True, stop=True)
                    last.then_inc(scores_ready, 1)

                def values(a):
                    wait(pe, logits_copied, a.n)
                    for i in range(NC):
                        last = mm(bank1[:, i * P:(i + 1) * P], h_t[:, i * P + 1:(i + 1) * P + 1], wwt[:],
                                  start=True, stop=True)
                    last.then_inc(values_ready, 1)

                def updates(a):
                    pe.wait_ge(wk_scaled, a.n + 1)
                    pe.wait_ge(values_copied, a.n + 1)
                    pe.wait_ge(scores_masked, a.n + 1)
                    for i in range(NC - 1):
                        last = mm(bank2[:, i * P:(i + 1) * P], wk_g[:, i * P:(i + 1) * P], v_sb[:, i * P:(i + 1) * P],
                                  start=True, stop=True)
                    last.then_inc(updates_ready, 1)

                def reads(a):
                    pe.wait_ge(states_ready, 2 * (a.n + 1))
                    wait(pe, combine_copied, a.n)
                    pe.wait_ge(rk_scaled, a.n + 1)
                    for i in range(NC):
                        cols = slice(i * P, (i + 1) * P)
                        if i:
                            mm(bank3[:, cols], state[:, i - 1, :], rk_g[:, (i - 1) * P:i * P], start=True, stop=False)
                        for h in range(H):
                            last = mm(bank3[h * DH:(h + 1) * DH, cols], v_sb[:, i * P + h * DH:i * P + (h + 1) * DH],
                                      kept[:, h, cols], start=(i == 0), stop=True)
                    last.then_inc(reads_ready, 1)

                def mix(a):
                    pe.wait_ge(reads_copied, a.n + 1)                 
                    pe.wait_ge(wrt_gated, a.n + 1)
                    for i in range(NC):
                        cols = slice(i * P, (i + 1) * P)
                        last = mm(bank0[:, cols], r_t[:, cols], wrt_g[:], start=True, stop=True)
                    last.then_inc(mixed_ready, 1)

                def turn_xhat2(a):
                    pe.wait_ge(normalized[1], a.n + 1)
                    turn_four(bank2, xhat[:, 1, :], xhat2_turned)

                def router(a):
                    pe.wait_ge(h2_ready, a.n + 1)
                    wait(pe, out_ready, a.n - 1)
                    for i in range(NC):
                        last = mm(bank1[:, i * E:(i + 1) * E], h2[:, i * P:(i + 1) * P], rwt[:], start=True, stop=True)
                    last.then_inc(logits_ready, 1)

                def turn_combine(a):
                    pe.wait_ge(combine_ready, a.n + 1)
                    if not last_one(a):
                        pe.wait_ge(scores_masked, a.n + 2)
                    turn(bank3[0:NC * E, 0:P], combine[:].rearrange("p c e -> p (c e)"),
                         ident[:]).then_inc(combine_turned, 1)

                def turn_weights(q):
                    bank, _, _ = blocks_of(q)
                    pe.wait_ge(w1_loaded if q < 4 else w2_loaded, 64)
                    wait(pe, weights_lo, q - 3)
                    for j in range(4):
                        eh = 4 * (q % 4) + j
                        src = w1_raw[:, eh, :] if q < 4 else w2_raw[:, eh // 2, (eh % 2) * P:(eh % 2 + 1) * P]
                        last = turn(bank[:, j * P:(j + 1) * P], src, ident[:])
                    last.then_inc(weights_turned, 1)

                late_parts = {(1, 1): (reads,), (2, 1): (mix,), (9, 2): (turn_xhat2,), (11, 1): (router,),
                              (14, 2): (turn_combine,)}
                early_parts = {(7, 1): (turn_xhat,), (12, 1): (scores,), (13, 0): (values,), (15, 2): (updates,)}
                ffn_parts = {(2, 2): (turn_ffn,)}

                def slot(b, late, early, f, prepare={}, busy={}):
                    for k in range(EH):
                        def parts(side):
                            do_parts(k, side, (f, ffn_parts), (late, late_parts), (early, early_parts))
                        parts(0)
                        if b is not None and k + 2 < EH:
                            w1_block(b, k + 2)
                        elif late is not None and b is not None and k + 2 >= EH:
                            w1_block(late, k + 2 - EH)
                        elif late is not None and b is None and k == START:
                            w1_block(late, 0)
                            w1_block(late, 1)
                        parts(1)
                        keep_busy(busy.get(k, 0), ps_y[1] if late is None or k < 2 else bank3)
                        for q in prepare.get(k, ()):
                            turn_weights(q)
                        if b is not None:
                            w2_block(b, k)
                        parts(2)

                pe.wait_ge(s_pool, 2)
                keep_busy(BUSY_FIRST)
                pe.wait_ge(silu_ready, 1)
                nc.tensor.transpose(bank3[:, NM * B:(NM + 1) * B], silu_c[:, 3, :], ident[0:B, 0:B]).then_inc(s_turn, 1)
                pe.wait_ge(s_wmod, 16)
                pe.wait_ge(silu_copied, 1)
                for j in range(NM):
                    last = nc.tensor.matmul(bank3[:, j * B:(j + 1) * B], wmod_sb[:, j * P:(j + 1) * P], silu_ct[:],
                                            start=True, stop=True)
                last.then_inc(s_turn, 1)

                run_slots(pe, slot)

            @block.scalar
            def _(act):
                def hidden(m, k):
                    s = EH * m.n + k
                    act.wait_ge(mid_ready, s + 1)
                    wait(act, g_lo_ready, s - 3)
                    nc.scalar.activation(g[:, k % 4, :], ps_mid[k % 2][:], ACT.Gelu,
                                         bias=b1t[:, k:k + 1]).then_inc(g_ready, 1)
                    wait(act, y_parts, s - 3)
                    nc.scalar.activation(g_hi[:, k % 4, :], ps_mid[k % 2][:], ACT.Gelu,
                                         bias=b1t[:, k:k + 1]).then_inc(g_hi_ready, 1)

                def modulated_h(a):
                    act.wait_ge(xhat_turned, a.n + 1)
                    act.wait_ge(cur_ready, a.n + 1)
                    wait(act, values_ready, a.n)
                    wait(act, rk_scaled, a.n)
                    nc.scalar.activation(h_t[:, 0:T], bank0[:], ACT.Identity, bias=cur[:, a.par, SA:SA + 1],
                                         scale=cur[:, a.par, CA:CA + 1]).then_inc(h_ready, 1)
                    if first(a):
                        act.wait_ge(gate_rows_turned, 1)
                        nc.scalar.activation(gate_rows_all[:], bank3[0:NG * B, P:2 * P], ACT.Copy).then_inc(gate_rows_copied, 1)
                        decay_powers()

                def decay_powers():
                    act.wait_ge(log_gamma_ready, 1)
                    act.wait_ge(lag_clipped, 1)
                    for h in range(H):
                        nc.scalar.activation(mask[:, h, :], lag[:], ACT.Exp, scale=loggam[:, h:h + 1]).then_inc(mask_powers, 1)
                    act.wait_ge(s_pool, 4)
                    for h in range(H):
                        nc.scalar.activation(wk_decay[:, :, h * DH:(h + 1) * DH],
                                             back[:].rearrange("p (a b) -> p a b", a=3), ACT.Exp,
                                             scale=loggam[:, h:h + 1])
                    nc.scalar.activation(rk_decay[:], steps[:], ACT.Exp, scale=loggam[:, H:H + 1])
                    nc.scalar.activation(chunk_decay[:], loggam[:, H:H + 1], ACT.Exp,
                                         scale=float(P)).then_inc(powers_ready, 1)

                def copy_values(a):
                    act.wait_ge(values_ready, a.n + 1)
                    wait(act, reads_ready, a.n)
                    nc.scalar.activation(v_sb[:], bank1[:], ACT.Copy).then_inc(values_copied, 1)

                def copy_reads(a):
                    act.wait_ge(reads_ready, a.n + 1)
                    wait(act, mixed_ready, a.n)
                    nc.scalar.activation(r_t[:, 1:T], bank3[:, 0:T - 1], ACT.Copy).then_inc(reads_copied, 1)
                    if first(a):
                        load_gelu()

                def modulated_h2(a):
                    act.wait_ge(xhat2_turned, a.n + 1)
                    wait(act, logits_ready, a.n)
                    wait(act, h2_lo_ready, a.n)
                    bias, scale = cur[:, a.par, SB:SB + 1], cur[:, a.par, CB:CB + 1]
                    nc.scalar.activation(h2[:], bank2[:], ACT.Identity, bias=bias, scale=scale).then_inc(h2_ready, 1)
                    wait(act, mid_ready, EH * (a.n - 1))
                    nc.scalar.activation(h2_hi[:, a.par, :], bank2[:], ACT.Identity, bias=bias,
                                         scale=scale).then_inc(h2_hi_ready, 1)

                def load_gelu():
                    nc.scalar.activation(gelu_warm[:], loggam[:], ACT.Gelu)

                def copy_combine(a):
                    act.wait_ge(combine_turned, a.n + 1)
                    wait(act, combine_stored, 16 * a.n)
                    nc.scalar.activation(combine_t[:], bank3[0:NC * E, 0:P], ACT.Copy).then_inc(combine_copied, 1)

                def weights_high(q):
                    bank, hi, _ = blocks_of(q)
                    act.wait_ge(weights_turned, q + 1)
                    nc.scalar.activation(hi, chunks(bank[:]), ACT.Copy).then_inc(weights_hi, 1)

                late_parts = {(1, 1): (copy_reads,), (9, 1): (modulated_h2,), (14, 1): (copy_combine,)}
                early_parts = {(7, 1): (modulated_h,), (13, 1): (copy_values,)}
                ffn_parts = {}

                def slot(b, late, early, f, prepare={}, busy={}):
                    for k in range(EH):
                        def parts(side):
                            do_parts(k, side, (f, ffn_parts), (late, late_parts), (early, early_parts))
                        parts(0)
                        if b is not None and k + 2 < EH:
                            hidden(b, k + 2)
                        elif late is not None and b is not None and k + 2 >= EH:
                            hidden(late, k + 2 - EH)
                        elif late is not None and b is None and k == START:
                            hidden(late, 0)
                            hidden(late, 1)
                        parts(1)
                        for q in prepare.get(k, ()):
                            weights_high(q)
                        parts(2)

                act.wait_ge(s_c, 16)
                nc.scalar.activation(silu_c[:, 0, :], c_sb[:], ACT.Exp, scale=-1.0).then_inc(exp_c_ready, 1)
                act.wait_ge(s_decay, 16 * N_DECAY)
                nc.scalar.activation(dtmp[:, 0, 0:H], decay_all[:], ACT.Exp, scale=-1.0)
                nc.scalar.activation(dtmp[:, 0, H:H + 1], decay_row[:], ACT.Exp, scale=-1.0)
                nc.scalar.activation(alpha_row[:], alpha_row[:], ACT.Exp).then_inc(exp_decay_ready, 1)
                act.wait_ge(gamma_ready, 1)
                nc.scalar.activation(loggam[:], dtmp[:, 2, :], ACT.Ln).then_inc(log_gamma_ready, 1)

                run_slots(act, slot)

            @block.vector
            def _(dve):
                tt, ts, stt = nc.vector.tensor_tensor, nc.vector.tensor_scalar, nc.vector.scalar_tensor_tensor

                def split(m, k):
                    s = EH * m.n + k
                    dve.wait_ge(g_hi_ready, s + 1)
                    wait(dve, y_parts, s - 3)
                    tt(g_lo[:, k % 4, :], g[:, k % 4, :], g_hi[:, k % 4, :].bitcast(F32),
                       ALU.subtract).then_inc(g_lo_ready, 1)

                def weigh(b, e):
                    dve.wait_ge(y_parts, EH * b.n + 2 * e + 2)
                    if e % EP == 0:
                        dve.wait_ge(combine_loaded[b.par][e // EP], 16 * (b.half + 1))
                    wait(dve, y_added, (E - 1) * b.n + {0: -1, 1: 0, 2: 1}.get(e, e - 2))
                    stt(out=chunks(y_w[:, e % 2, :]), in0=chunks(ps_y[e % 2][:]), scalar=b2t[:, e:e + 1],
                        in1=combine_all[:, b.par, :, e, :], op0=ALU.add, op1=ALU.mult).then_inc(y_weighted, 1)

                def statistics(a, which, src):
                    for i in range(NC):
                        last = nc.vector.bn_stats(stats[:, which, i, :], src[:, i * P:(i + 1) * P])
                    last.then_inc(ln_stats[which], 1)

                def aggregate(a, which):
                    dve.wait_ge(ln_stats[which], a.n + 1)
                    wait(dve, normalized[which], a.n)
                    stand_alone(dve, dve_passed)
                    for i in range(NC):
                        last = nc.vector.bn_aggr(moments[:, which, i, :], stats[:, which, i, :])
                    last.then_inc(ln_moments[which], 1)

                def start(a):
                    if not first(a):
                        first_statistics(a)

                def first_statistics(a):
                    dve.wait_ge(x_loaded[a.par], 16 * (a.half + 1))
                    statistics(a, 0, x_in[:, a.par, :])

                def aggregate_x(a):
                    if not first(a):
                        aggregate(a, 0)

                def pick_modulation(a):
                    if first(a):
                        modulation()
                    wait(dve, h2_hi_ready, a.n - 1)
                    nc.vector.tensor_copy(cur[:, a.par, :], mods[:, a.n, :]).then_inc(cur_ready, 1)
                    if first(a):
                        gate_columns()
                        small_weights()

                def mask_scores(a):
                    dve.wait_ge(scores_ready, a.n + 1)
                    if first(a):
                        dve.wait_ge(s_mask, H)
                        dve.wait_ge(powers_ready, 1)
                    wait(dve, reads_ready, a.n)
                    tt(kept[:, 0, :], bank2[:], mask[:, 0, :], ALU.mult)
                    tt(kept[:, 1, :], bank3[:], mask[:, 1, :], ALU.mult).then_inc(scores_masked, 1)

                def scale_wk(a):
                    dve.wait_ge(h_tok_step, 2 * (a.n + 1))
                    wait(dve, updates_ready, a.n)
                    tt(chunks(wk_g[:]), chunks(h_tok[:, 0:3 * P]), wk_decay[:], ALU.mult).then_inc(wk_scaled, 1)

                def states(a):
                    dve.wait_ge(updates_ready, a.n + 1)
                    wait(dve, reads_ready, a.n)
                    tt(state[:], chunks(bank2[:, 0:3 * P]), same_head[:], ALU.mult).then_inc(updates_masked, 1)
                    dve.wait_ge(updates_masked, a.n + 1)
                    for i in (1, 2):
                        stt(out=state[:, i, :], in0=state[:, i - 1, :], scalar=chunk_decay[:], in1=state[:, i, :],
                            op0=ALU.mult, op1=ALU.add).then_inc(states_ready, 1)
                        dve.wait_ge(states_ready, 2 * a.n + i)

                def residual(a):
                    dve.wait_ge(mixed_ready, a.n + 1)
                    dve.wait_ge(base_step, 2 * (a.n + 1))
                    wait(dve, out_ready, a.n - 1)
                    tt(x1[:, a.par, :], x_base[:], bank0[:], ALU.add).then_inc(x1_ready, 1)

                def statistics_x1(a):
                    dve.wait_ge(x1_ready, a.n + 1)
                    statistics(a, 1, x1[:, a.par, :])

                def aggregate_x1(a):
                    aggregate(a, 1)

                def route(a):
                    done = ROUTER_STEPS * a.n
                    dve.wait_ge(logits_ready, a.n + 1)
                    nc.vector.tensor_copy(logits[:], bank1[:, 0:NC * E].rearrange("p (c e) -> p c e", e=E)).then_inc(logits_copied, 1)
                    dve.wait_ge(logits_copied, a.n + 1)
                    wait(dve, gap_ready, a.n)
                    stand_alone(dve, dve_passed)
                    for i in range(NC):
                        last = nc.vector.max(top_val[:, i, :], logits[:, i, :])
                    last.then_inc(router_step, 1)
                    dve.wait_ge(router_step, done + 1)
                    wait(dve, gap_exp_ready, a.n)
                    tt(gap[:], top_val[:, :, 1], top_val[:, :, 0], ALU.subtract).then_inc(gap_ready, 1)

                def route_indices(a):
                    done = ROUTER_STEPS * a.n
                    for i in range(NC):
                        last = nc.vector.max_index(top_idx[:, i, :], top_val[:, i, :], logits[:, i, :])
                    last.then_inc(router_step, 1)
                    dve.wait_ge(router_step, done + 2)
                    nc.vector.tensor_copy(top_f[:], top_idx[:, :, 0:2]).then_inc(router_step, 1)
                    dve.wait_ge(router_step, done + 3)
                    for j in range(2):
                        last = tt(hot[:, j, :, :], expert_ids[:], top_f[:, :, j:j + 1].to_broadcast([P, NC, E]), ALU.is_equal)
                    last.then_inc(router_step, 1)

                def route_end(a):
                    done = ROUTER_STEPS * a.n
                    dve.wait_ge(gap_exp_ready, a.n + 1)
                    ts(gap_sum[:], gap_exp[:], 1.0, None, ALU.add).then_inc(router_step, 1)
                    dve.wait_ge(router_step, done + 5)
                    nc.vector.reciprocal(probs[:, 0, :], gap_sum[:]).then_inc(router_step, 1)
                    dve.wait_ge(router_step, done + 6)
                    tt(probs[:, 1, :], probs[:, 0, :], gap_exp[:], ALU.mult).then_inc(router_step, 1)
                    dve.wait_ge(router_step, done + 7)
                    for j in range(2):
                        last = tt(hot[:, j, :, :], hot[:, j, :, :],
                                  probs[:, j, :].unsqueeze(2).to_broadcast([P, NC, E]), ALU.mult)
                    last.then_inc(hot_scaled, 1)
                    dve.wait_ge(hot_scaled, a.n + 1)
                    wait(dve, combine_turned, a.n)
                    tt(combine[:], hot[:, 0, :, :], hot[:, 1, :, :], ALU.add).then_inc(combine_ready, 1)

                def weigh_last(f):
                    weigh(f, E - 1)

                def scale_ffn(f):
                    dve.wait_ge(y_added, (E - 1) * (f.n + 1))
                    ts(f_t[:], y_sum[:], mods[:, f.n, GB:GB + 1], None, ALU.mult).then_inc(f_scaled, 1)

                def finish(f):
                    dve.wait_ge(ffn_turned, f.n + 1)
                    wait(dve, out_stored[f.par], 16 * f.half)
                    tt(out_sb[:, f.par, :], x1[:, f.par, :], bank1[:], ALU.add).then_inc(out_ready, 1)

                def modulation():
                    dve.wait_ge(s_turn, 2)
                    nc.vector.tensor_copy(mods[:].rearrange("p b j -> p j b"),
                                          bank3[:, 0:NM * B].rearrange("p (j b) -> p j b", j=NM)).then_inc(s_dve0, 1)
                    dve.wait_ge(s_dve0, 5)
                    for j in (CA, CB):
                        nc.vector.tensor_scalar(mods[:, :, j], mods[:, :, j], 1.0, None, ALU.add)
                    gates = ((0, GA), (1, GB))
                    for i, j in gates:
                        nc.vector.tensor_scalar(gate_tmp[:, i, 0, :], mods[:, :, j], -1.0, None, ALU.mult)
                        last = nc.vector.tensor_scalar(gate_tmp[:, i, 1, :], mods[:, :, j], 0.0, 2.0, ALU.is_ge, ALU.mult)
                    last.then_inc(s_dve0, 1)
                    dve.wait_ge(s_dve0, 6)
                    for i, j in gates:
                        last = nc.vector.tensor_tensor(gate_tmp[:, i, 2, :], gate_tmp[:, i, 0, :], mods[:, :, j], ALU.max)
                    last.then_inc(s_dve0, 1)
                    dve.wait_ge(s_dve0, 7)
                    for i, j in gates:
                        last = nc.vector.tensor_scalar(gate_tmp[:, i, 3, :], gate_tmp[:, i, 2, :], GATE_FLOOR, None, ALU.max)
                    last.then_inc(s_dve0, 1)
                    dve.wait_ge(s_dve0, 8)
                    for i, j in gates:
                        last = nc.vector.scalar_tensor_tensor(out=mods[:, :, j], in0=gate_tmp[:, i, 1, :], scalar=-1.0,
                                                              in1=gate_tmp[:, i, 3, :], op0=ALU.add, op1=ALU.mult)
                    last.then_inc(s_dve0, 1)
                    dve.wait_ge(s_dve0, 9)

                def gate_columns():
                    for j, part in enumerate((GA, CA, SA)):
                        last = nc.vector.tensor_copy(gate_cols[:, j, :], mods[:, :, part])
                    last.then_inc(gate_cols_ready, 1)

                def small_weights():
                    dve.wait_ge(s_turn, 3)
                    nc.vector.tensor_copy(wwt[:], bank2[:, 0:P])
                    nc.vector.tensor_scalar(wrt[:], bank2[:, P:2 * P], alpha_row[:], None, ALU.mult)
                    nc.vector.tensor_copy(rwt[:], bank2[:, 256:256 + E])
                    nc.vector.tensor_copy(b1t[:], bank2[:, 272:272 + EH])
                    nc.vector.tensor_copy(b2t[:], bank2[:, 288:288 + E]).then_inc(small_ready, 1)

                def weights_low(q):
                    bank, hi, lo = blocks_of(q)
                    dve.wait_ge(weights_hi, q + 1)
                    tt(lo, chunks(bank[:]), hi.bitcast(F32), ALU.subtract).then_inc(weights_lo, 1)

                late_parts = {(3, 2): (residual,), (5, 1): (statistics_x1,), (6, 1): (aggregate_x1,),
                              (11, 1): (route,), (13, 1): (route_indices, route_end,)}
                early_parts = {(0, 2): (start,), (1, 1): (aggregate_x,), (6, 1): (pick_modulation,),
                               (13, 1): (mask_scores,), (14, 2): (scale_wk,), (15, 1): (states,)}
                ffn_parts = {(0, 0): (weigh_last,), (2, 0): (scale_ffn,), (3, 1): (finish,)}

                weigh_at = {2: 0, 4: 1, 6: 2, 8: 3, 10: 4, 12: 5, 14: 6}

                def slot(b, late, early, f, prepare={}, busy={}):
                    for k in range(EH):
                        def parts(side):
                            do_parts(k, side, (f, ffn_parts), (late, late_parts), (early, early_parts))
                        parts(0)
                        if b is not None and k + 1 < EH:
                            split(b, k + 1)
                        elif late is not None and k + 1 == EH:
                            split(late, 0)
                        parts(1)
                        if b is not None and k in weigh_at:
                            weigh(b, weigh_at[k])
                        parts(2)
                        for q in prepare.get(k, ()):
                            weights_low(q)

                nc.vector.memset(h_t[:, T:T + 1], 0.0)
                nc.vector.memset(r_t[:, 0:1], 0.0)
                nc.vector.memset(same_head[:], 0.0).then_inc(s_dve0, 1)
                dve.wait_ge(s_dve0, 1)
                for h in range(H):
                    nc.vector.memset(same_head[h * DH:(h + 1) * DH, :, h * DH:(h + 1) * DH], 1.0)
                dve.wait_ge(exp_c_ready, 1)
                nc.vector.tensor_scalar(silu_c[:, 1, :], silu_c[:, 0, :], 1.0, None, ALU.add).then_inc(s_dve0, 1)
                dve.wait_ge(s_dve0, 2)
                nc.vector.reciprocal(silu_c[:, 2, :], silu_c[:, 1, :]).then_inc(s_dve0, 1)
                dve.wait_ge(s_dve0, 3)
                nc.vector.tensor_tensor(silu_c[:, 3, :], silu_c[:, 2, :], c_sb[:], ALU.mult).then_inc(silu_ready, 1)
                first_statistics(Batch(0, 0))
                dve.wait_ge(s_turn, 1)
                nc.vector.tensor_copy(silu_ct[:], bank3[:, NM * B:(NM + 1) * B]).then_inc(silu_copied, 1)
                aggregate(Batch(0, 0), 0)
                dve.wait_ge(exp_decay_ready, 1)
                nc.vector.tensor_scalar(dtmp[:, 1, :], dtmp[:, 0, :], 1.0, None, ALU.add).then_inc(s_dve0, 1)
                dve.wait_ge(s_dve0, 4)
                nc.vector.reciprocal(dtmp[:, 2, :], dtmp[:, 1, :]).then_inc(gamma_ready, 1)
                dve.wait_ge(s_pool, 3)
                nc.vector.tensor_scalar(lag[:], lag[:], 0.0, None, ALU.max).then_inc(lag_clipped, 1)

                run_slots(dve, slot)

            @block.gpsimd
            def _(pool):
                def add_last(f):
                    add_y(f, E - 1)

                def normalize(a, which, src, turned):
                    pool.wait_ge(ln_moments[which], a.n + 1)
                    nc.gpsimd.tensor_tensor(var_eps[:, which, :], moments[:, which, :, 1], eps_tile[:],
                                            ALU.add).then_inc(eps_added[which], 1)
                    pool.wait_ge(eps_added[which], a.n + 1)
                    nc.gpsimd.tensor_tensor(rstd[:, which, :], var_eps[:, which, :], minus_half[:], ALU.pow)
                    wait(pool, turned, a.n)
                    if which == 0:
                        wait(pool, h_tok_step, 2 * a.n)
                    nc.gpsimd.tensor_tensor(minus_mean[:, which, :], zeros[:], moments[:, which, :, 0],
                                            ALU.subtract).then_inc(rstd_ready[which], 1)
                    pool.wait_ge(rstd_ready[which], a.n + 1)
                    stand_alone(pool, pool_passed)
                    for i in range(NC):
                        last = nc.gpsimd.tensor_scalar(xhat[:, which, i * P:(i + 1) * P], src[:, i * P:(i + 1) * P],
                                                       minus_mean[:, which, i:i + 1], rstd[:, which, i:i + 1],
                                                       ALU.add, ALU.mult)
                    last.then_inc(normalized[which], 1)

                def normalize_x(a):
                    normalize(a, 0, x_in[:, a.par, :], xhat_turned)

                def normalize_x1(a):
                    normalize(a, 1, x1[:, a.par, :], xhat2_turned)

                def split_h2(a):
                    pool.wait_ge(h2_hi_ready, a.n + 1)
                    wait(pool, mid_ready, EH * (a.n - 1))
                    nc.gpsimd.tensor_tensor(h2_lo[:, a.par, :], h2[:], h2_hi[:, a.par, :].bitcast(F32),
                                            ALU.subtract).then_inc(h2_lo_ready, 1)

                def triangle():
                    for h in range(H):
                        pool.wait_ge(mask_powers, h + 1)
                        nc.gpsimd.affine_select(out=mask[:, h, :], in_=mask[:, h, :], compare_op=ALU.is_gt, fill=0.0,
                                                base=0, pattern=[[0, NC], [1, P]], channel_multiplier=-1).then_inc(s_mask, 1)

                def scale_h(a):
                    pool.wait_ge(h_ready, a.n + 1)
                    if first(a):
                        triangle()
                        pool.wait_ge(powers_ready, 1)
                    wait(pool, reads_ready, a.n)
                    nc.gpsimd.tensor_tensor(rk_g[:], h_t[:, 1 + P:1 + T], rk_decay[:], ALU.mult).then_inc(rk_scaled, 1)

                def gate_read(a):
                    pool.wait_ge(rows_loaded[a.par], 16 * (a.half + 1))
                    wait(pool, mixed_ready, a.n)
                    if first(a):
                        pool.wait_ge(small_ready, 1)
                    nc.gpsimd.tensor_tensor(wrt_g[:], wrt[:], gate_rows[:, a.par, 0, :], ALU.mult).then_inc(wrt_gated, 1)

                def row(a, j):
                    return gate_rows[:, a.par, j, :].unsqueeze(1).to_broadcast([P, NC, P])

                def modulate_tokens(a):
                    pool.wait_ge(rows_loaded[a.par], 16 * (a.half + 1))
                    pool.wait_ge(normalized[0], a.n + 1)
                    wait(pool, wk_scaled, a.n)
                    wait(pool, base_step, 2 * a.n)
                    nc.gpsimd.tensor_tensor(chunks(h_tok[:]), chunks(xhat[:, 0, :]), row(a, 1), ALU.mult).then_inc(h_tok_step, 1)
                    pool.wait_ge(h_tok_step, 2 * a.n + 1)
                    nc.gpsimd.tensor_tensor(chunks(h_tok[:]), chunks(h_tok[:]), row(a, 2), ALU.add).then_inc(h_tok_step, 1)

                def base_x(a):
                    wait(pool, x1_ready, a.n)
                    pool.wait_ge(h_tok_step, 2 * (a.n + 1))
                    nc.gpsimd.tensor_tensor(chunks(x_base[:]), chunks(h_tok[:]), row(a, 0), ALU.mult).then_inc(base_step, 1)
                    pool.wait_ge(base_step, 2 * a.n + 1)
                    nc.gpsimd.tensor_tensor(x_base[:], x_base[:], x_in[:, a.par, :], ALU.add).then_inc(base_step, 1)

                def exp_gap(a):
                    pool.wait_ge(gap_ready, a.n + 1)
                    wait(pool, combine_ready, a.n)
                    nc.gpsimd.tensor_tensor(gap_exp[:], e_base[:], gap[:], ALU.pow).then_inc(gap_exp_ready, 1)

                def add_y(b, e):
                    n = (E - 1) * b.n + e
                    pool.wait_ge(y_weighted, E * b.n + e + 1)
                    if e == 1:
                        wait(pool, f_scaled, b.n)
                        nc.gpsimd.tensor_tensor(y_sum[:], y_w[:, 0, :], y_w[:, 1, :], ALU.add).then_inc(y_added, 1)
                    else:
                        pool.wait_ge(y_added, n - 1)
                        nc.gpsimd.tensor_tensor(y_sum[:], y_sum[:], y_w[:, e % 2, :], ALU.add).then_inc(y_added, 1)

                late_parts = {(6, 0): (normalize_x1,), (9, 1): (split_h2,), (11, 0): (exp_gap,)}
                early_parts = {(1, 1): (normalize_x,), (11, 1): (scale_h,), (12, 0): (modulate_tokens,),
                               (14, 0): (gate_read,), (14, 1): (base_x,)}
                ffn_parts = {(0, 1): (add_last,)}

                add_at = {4: 1, 6: 2, 8: 3, 10: 4, 12: 5, 14: 6}

                def slot(b, late, early, f, prepare={}, busy={}):
                    for k in range(EH):
                        def parts(side):
                            do_parts(k, side, (f, ffn_parts), (late, late_parts), (early, early_parts))
                        parts(0)
                        if b is not None and k in add_at:
                            add_y(b, add_at[k])
                        parts(1)
                        parts(2)

                nc.gpsimd.memset(ones[:], 1.0).then_inc(s_pool, 1)
                nc.gpsimd.memset(minus_half[:], -0.5)
                nc.gpsimd.memset(eps_tile[:], EPS)
                nc.gpsimd.memset(zeros[:], 0.0)
                nc.gpsimd.memset(e_base[:], E_CONST)
                pool.wait_ge(s_pool, 1)
                nc.gpsimd.affine_select(out=ident[:], in_=ones[:], compare_op=ALU.is_equal, fill=0.0, base=0,
                                        pattern=[[-1, P]], channel_multiplier=1).then_inc(s_pool, 1)
                nc.gpsimd.iota(lag[:], pattern=[[0, NC], [1, P]], base=-1, channel_multiplier=-1,
                               allow_small_or_imprecise_dtypes=True).then_inc(s_pool, 1)
                nc.gpsimd.iota(steps[:], pattern=[[0, 3], [1, P]], base=0, channel_multiplier=0,
                               allow_small_or_imprecise_dtypes=True)
                nc.gpsimd.iota(back[:], pattern=[[0, 3 * DH]], base=P - 1, channel_multiplier=-1,
                               allow_small_or_imprecise_dtypes=True)
                nc.gpsimd.iota(expert_ids[:], pattern=[[0, NC], [1, E]], base=0, channel_multiplier=0,
                               allow_small_or_imprecise_dtypes=True).then_inc(s_pool, 1)
                pool.wait_ge(s_pool, 4)

                run_slots(pool, slot)


_INS = ["L0_attn_out", "L0_attn_W_write", "L0_attn_W_read", "L0_attn_decay", "L0_attn_log_alpha",
        "L0_ffn_router_w", "L0_ffn_w1", "L0_ffn_b1", "L0_ffn_w2", "L0_ffn_b2", "L0_c", "L0_wmod"]


def kernel(**inputs):
    import numpy as np
    import concourse.bacc as bacc
    from concourse.bass_utils import run_bass_kernel_spmd

    nc = bacc.Bacc("TRN2", target_bir_lowering=False, num_devices=1)
    arrays, args = {}, []
    for name in _INS:
        a = np.ascontiguousarray(inputs[name])
        arrays[f"in_{name}"] = a
        args.append(nc.dram_tensor(f"in_{name}", a.shape, mybir.dt.from_np(a.dtype), kind="ExternalInput").ap())
    shape = inputs["L0_attn_out"].shape
    out = nc.dram_tensor("out_0", shape, F32, kind="ExternalOutput").ap()
    adaln_retention_moe(nc, *args, out)
    r = run_bass_kernel_spmd(nc, [arrays], core_ids=[0])
    return r.results[0]["out_0"]
```
